# Optimizing a Trainium2 kernel written in Bass

```python
import numpy as np
import jax
import jax.numpy as jnp

def _softmax(x, axis=-1):
    return jax.nn.softmax(x, axis=axis)

def _gelu(x):
    return jax.nn.gelu(x, approximate=True)

def _silu(x):
    return jax.nn.silu(x)

def _sigmoid(x):
    return jax.nn.sigmoid(x)

def _layernorm(x, axis=-1, eps=1e-05):
    m = jnp.mean(x, axis=axis, keepdims=True)
    v = jnp.var(x, axis=axis, keepdims=True)
    return (x - m) / jnp.sqrt(v + eps)

def _scatter_add(tgt, idx, src, axis=0):
    return tgt.at[idx].add(src)

def _segment_sum(src, seg, n):
    return jax.ops.segment_sum(src, seg, n)
kernel_name = 'mk_seq_postln_d1_jaxref_r8_74b03e'

def setup_inputs(seed: int=0):
    np.random.seed(seed)
    _w = jnp.asarray

    def _L0_attn_setup():
        import jax, jax.numpy as jnp
        import numpy as np
        B, N, C, H = (4, 512, 128, 16)
        D = C // H
        LN_EPS = 1e-05
        key = jax.random.key(seed)
        ks = jax.random.split(key, 20)
        s = 0.02
        inp = {'x': jax.random.normal(ks[0], (B, N, C), jnp.float32)}
        for i, nm in enumerate(['q', 'k1', 'k2', 'v1', 'v2']):
            inp[f'W{nm}'] = jax.random.normal(ks[1 + i], (C, C), jnp.float32) * s
            inp[f'b{nm}'] = jnp.zeros((C,), jnp.float32)
        for i in range(4):
            inp[f'g{i + 1}'] = jax.random.normal(ks[10 + i], (H,), jnp.float32) * 0.5
        inp['ln_g'] = jnp.ones((C,), jnp.float32)
        inp['ln_b'] = jnp.zeros((C,), jnp.float32)
        inp['Wo'] = jax.random.normal(ks[14], (C, C), jnp.float32) * s
        inp['bo'] = jnp.zeros((C,), jnp.float32)
        return inp
    _L0_attn_in = _L0_attn_setup()

    def _L0_ffn_setup():
        import jax, jax.numpy as jnp
        import numpy as np
        B, S, D, F, E = (2, 256, 128, 512, 8)
        LN_EPS = 1e-05

        def _xavier(key, shape, fan_in, fan_out):
            a = np.sqrt(6.0 / (fan_in + fan_out))
            return jax.random.uniform(key, shape, jnp.float32, -a, a)
        key = jax.random.key(seed)
        ks = jax.random.split(key, 8)
        tgt = jax.random.normal(ks[0], (B, S, D), jnp.float32)
        router_w = _xavier(ks[1], (E, D), D, E)
        router_b = jnp.zeros((E,), jnp.float32)
        w1 = _xavier(ks[2], (E, D, F), D, F)
        b1 = jnp.zeros((E, F), jnp.float32)
        w2 = _xavier(ks[3], (E, F, D), F, D)
        b2 = jnp.zeros((E, D), jnp.float32)
        gamma = jnp.ones((D,), jnp.float32)
        beta = jnp.zeros((D,), jnp.float32)
        return {'tgt': tgt, 'router_w': router_w, 'router_b': router_b, 'w1': w1, 'b1': b1, 'w2': w2, 'b2': b2, 'gamma': gamma, 'beta': beta}
    _L0_ffn_in = _L0_ffn_setup()
    _d = {'L0_attn_x': _L0_attn_in['x'], 'L0_attn_Wq': _L0_attn_in['Wq'], 'L0_attn_bq': _L0_attn_in['bq'], 'L0_attn_Wk1': _L0_attn_in['Wk1'], 'L0_attn_bk1': _L0_attn_in['bk1'], 'L0_attn_Wk2': _L0_attn_in['Wk2'], 'L0_attn_bk2': _L0_attn_in['bk2'], 'L0_attn_Wv1': _L0_attn_in['Wv1'], 'L0_attn_bv1': _L0_attn_in['bv1'], 'L0_attn_Wv2': _L0_attn_in['Wv2'], 'L0_attn_bv2': _L0_attn_in['bv2'], 'L0_attn_g1': _L0_attn_in['g1'], 'L0_attn_g2': _L0_attn_in['g2'], 'L0_attn_g3': _L0_attn_in['g3'], 'L0_attn_g4': _L0_attn_in['g4'], 'L0_attn_ln_g': _L0_attn_in['ln_g'], 'L0_attn_ln_b': _L0_attn_in['ln_b'], 'L0_attn_Wo': _L0_attn_in['Wo'], 'L0_attn_bo': _L0_attn_in['bo'], 'L0_ffn_router_w': _L0_ffn_in['router_w'], 'L0_ffn_router_b': _L0_ffn_in['router_b'], 'L0_ffn_w1': _L0_ffn_in['w1'], 'L0_ffn_b1': _L0_ffn_in['b1'], 'L0_ffn_w2': _L0_ffn_in['w2'], 'L0_ffn_b2': _L0_ffn_in['b2'], 'L0_ffn_gamma': _L0_ffn_in['gamma'], 'L0_ffn_beta': _L0_ffn_in['beta']}
    _x0 = _d['L0_attn_x']
    _d['L0_attn_x'] = jax.random.normal(jax.random.fold_in(jax.random.key(seed), 1), (8, 1024, 128), dtype=_x0.dtype)
    del _x0
    return _d

def reference(L0_attn_x, L0_attn_Wq, L0_attn_bq, L0_attn_Wk1, L0_attn_bk1, L0_attn_Wk2, L0_attn_bk2, L0_attn_Wv1, L0_attn_bv1, L0_attn_Wv2, L0_attn_bv2, L0_attn_g1, L0_attn_g2, L0_attn_g3, L0_attn_g4, L0_attn_ln_g, L0_attn_ln_b, L0_attn_Wo, L0_attn_bo, L0_ffn_router_w, L0_ffn_router_b, L0_ffn_w1, L0_ffn_b1, L0_ffn_w2, L0_ffn_b2, L0_ffn_gamma, L0_ffn_beta):

    def _L0_attn_ref(x, Wq, bq, Wk1, bk1, Wk2, bk2, Wv1, bv1, Wv2, bv2, g1, g2, g3, g4, ln_g, ln_b, Wo, bo):
        import jax, jax.numpy as jnp
        import numpy as np
        B, N, C, H = (4, 512, 128, 16)
        D = C // H
        LN_EPS = 1e-05
        b, n, c = x.shape
        h, d = (H, c // H)

        def proj_heads(W, bb):
            z = x + x @ W.T + bb
            return z.reshape(b, n, h, d).transpose(0, 2, 1, 3)
        q = proj_heads(Wq, bq).astype(jnp.float32)
        k1 = proj_heads(Wk1, bk1).astype(jnp.float32)
        k2 = proj_heads(Wk2, bk2).astype(jnp.float32)
        v1 = proj_heads(Wv1, bv1).astype(jnp.float32)
        v2 = proj_heads(Wv2, bv2).astype(jnp.float32)
        S1 = jnp.einsum('bhnd,bhne->bhde', k1, v1) / n
        S2 = jnp.einsum('bhnd,bhne->bhde', k2, v2) / n
        v1m = v1.mean(axis=2, keepdims=True)
        v2m = v2.mean(axis=2, keepdims=True)
        S12 = S1 * S2
        y1 = q @ S1 * v2m
        y2 = S12.sum(axis=2, keepdims=True)
        y3 = q @ S2 * v1m
        y4 = q @ S12
        gr = lambda g: g.reshape(1, h, 1, 1)
        out = y1 * gr(g1) + y2 * gr(g2) + y3 * gr(g3) + y4 * gr(g4)
        out = out.transpose(0, 2, 1, 3).reshape(b, n, c)
        mu = out.mean(axis=-1, keepdims=True)
        var = jnp.mean((out - mu) ** 2, axis=-1, keepdims=True)
        out = (out - mu) * jax.lax.rsqrt(var + LN_EPS) * ln_g + ln_b
        return out @ Wo.T + bo

    def _L0_ffn_ref(tgt, router_w, router_b, w1, b1, w2, b2, gamma, beta):
        import jax, jax.numpy as jnp
        import numpy as np
        B, S, D, F, E = (2, 256, 128, 512, 8)
        LN_EPS = 1e-05

        def _xavier(key, shape, fan_in, fan_out):
            a = np.sqrt(6.0 / (fan_in + fan_out))
            return jax.random.uniform(key, shape, jnp.float32, -a, a)
        logits = jnp.einsum('bsd,ed->bse', tgt, router_w) + router_b
        rw = jax.nn.softmax(logits, axis=-1)
        rw = jnp.zeros_like(rw).at[..., 0].set(1.0)
        h = jax.nn.relu(jnp.einsum('bsd,edf->besf', tgt, w1) + b1[None, :, None, :])
        eo = jnp.einsum('besf,efd->besd', h, w2) + b2[None, :, None, :]
        tgt2 = jnp.einsum('besd,bse->bsd', eo, rw)
        x = tgt + tgt2
        mean = jnp.mean(x, axis=-1, keepdims=True)
        var = jnp.mean(jnp.square(x - mean), axis=-1, keepdims=True)
        return (x - mean) * jax.lax.rsqrt(var + LN_EPS) * gamma + beta
    x = L0_attn_x
    x = _layernorm(x + _L0_attn_ref(x, L0_attn_Wq, L0_attn_bq, L0_attn_Wk1, L0_attn_bk1, L0_attn_Wk2, L0_attn_bk2, L0_attn_Wv1, L0_attn_bv1, L0_attn_Wv2, L0_attn_bv2, L0_attn_g1, L0_attn_g2, L0_attn_g3, L0_attn_g4, L0_attn_ln_g, L0_attn_ln_b, L0_attn_Wo, L0_attn_bo), axis=-1)
    x = _layernorm(x + _L0_ffn_ref(x, L0_ffn_router_w, L0_ffn_router_b, L0_ffn_w1, L0_ffn_b1, L0_ffn_w2, L0_ffn_b2, L0_ffn_gamma, L0_ffn_beta), axis=-1)
    return x

_drawn_inputs = setup_inputs


def setup_inputs(seed=0):
    import zlib

    import numpy as np

    out = dict(_drawn_inputs(seed))
    spreads = {'L0_attn_bq': (0.0, 0.665),
     'L0_attn_bk1': (0.0, 0.8),
     'L0_attn_bk2': (0.0, 0.8),
     'L0_attn_bv1': (0.0, 0.612),
     'L0_attn_bv2': (0.0, 0.501),
     'L0_attn_ln_g': (1.0, 0.2),
     'L0_attn_ln_b': (0.0, 0.33),
     'L0_attn_bo': (0.0, 0.1),
     'L0_ffn_router_b': (0.0, 0.1),
     'L0_ffn_b1': (0.0, 0.1),
     'L0_ffn_b2': (0.0, 0.1),
     'L0_ffn_gamma': (1.0, 0.2),
     'L0_ffn_beta': (0.0, 0.1)}
    factors = {'L0_attn_Wk1': 8.0,
     'L0_attn_Wk2': 8.0,
     'L0_attn_Wv1': 8.0,
     'L0_attn_Wv2': 8.0,
     'L0_attn_g1': 3.019,
     'L0_attn_g3': 4.05}
    for name, (base, spread) in spreads.items():
        noise = np.random.default_rng([zlib.crc32(name.encode()), seed]).standard_normal(out[name].shape)
        drawn = base * np.exp(spread * noise) if base else spread * noise
        out[name] = jnp.asarray(drawn.astype(out[name].dtype))
    for name, factor in factors.items():
        out[name] = (out[name] * factor).astype(out[name].dtype)
    return out
```

```python
from contextlib import ExitStack

import concourse.bass as bass
from concourse import mybir

BATCHES, SEQ, C, HEADS, FF = 8, 1024, 128, 16, 512
HEAD = C // HEADS
EPS = 1e-5
TILE = 128
SEQ_TILES = SEQ // TILE
TILES = 4
GROUP = TILES * TILE
SEQ_GROUPS = SEQ // GROUP
GROUPS = BATCHES * SEQ_GROUPS
FCH = FF // 128
XW = C + 2
PERIOD = 4


def build(nc, x, Wq, bq, Wk1, bk1, Wk2, bk2, Wv1, bv1, Wv2, bv2, g1, g2, g3, g4, ln_g, ln_b, Wo, bo,
          w1, b1, w2, b2, gamma, beta, out):
    f32 = mybir.dt.float32
    ALU = mybir.AluOpType
    ACT = mybir.ActivationFunctionType

    x_v = x.rearrange("b (p t) c -> b p t c", t=SEQ_TILES)
    out_v = out.rearrange("b (p t) c -> b p t c", t=SEQ_TILES)

    ctx = ExitStack()
    with ctx:
        def sb(name, shape):
            return ctx.enter_context(nc.sbuf_tensor(name, shape, f32))

        def bank(name):
            return ctx.enter_context(nc.psum_tensor(name, [128, 512], f32))

        def sem(name):
            return ctx.enter_context(nc.semaphore(name))

        ident = sb("ident", [128, 128])
        ones = sb("ones", [128, 128])
        center = sb("center", [128, 128])
        inv_c = sb("inv_c", [128, 1])
        head_mask = sb("head_mask", [128, 128])
        w_raw = sb("w_raw", [128, 6, 128])
        AqT = sb("AqT", [128, XW])
        Ak = sb("Ak", [128, 2, 128])
        Av = sb("Av", [128, 3, 128])
        WoT = sb("WoT", [128, 128])
        Wog = sb("Wog", [128, 128])
        bv_rows = sb("bv_rows", [128, 3, 128])
        nbv_rows = sb("nbv_rows", [128, 2, 128])
        cols = sb("cols", [128, 4])
        gcols = sb("gcols", [128, 4])
        gmask = sb("gmask", [128, 4, 128])
        lnb_wide = sb("lnb_wide", [128, 128])
        bo_rows = sb("bo_rows", [128, 128])
        u_rows = sb("u_rows", [128, 128])
        w1_sb = sb("w1_sb", [128, FF])
        b1_sb = sb("b1_sb", [128, FCH])
        w2_sb = sb("w2_sb", [128, FCH, C])
        b2_rows = sb("b2_rows", [128, C])
        gamma_rows = sb("gamma_rows", [128, C])
        beta_rows = sb("beta_rows", [128, C])
        eps_col = sb("eps_col", [128, 1])

        X = [sb(f"X{i}", [128, SEQ_TILES, XW]) for i in range(2)]
        G_sb = sb("G_sb", [128, XW])
        E_sb = sb("E_sb", [128, 2, 128])
        V_sb = sb("V_sb", [128, 2, 128])
        S_sb = sb("S_sb", [128, 2, 128])
        gv = sb("gv", [128, 2, 128])
        T_sb = sb("T_sb", [128, 2, 128])
        S12 = sb("S12", [128, 128])
        S12g = sb("S12g", [128, 2, 128])
        M_half = sb("M_half", [128, 128])
        M_sb = sb("M_sb", [128, 128])
        PT_sb = sb("PT_sb", [128, XW])
        P_sb = sb("P_sb", [128, XW])

        xT = sb("xT", [128, GROUP])
        zT = sb("zT", [128, GROUP])
        zT_sq = sb("zT_sq", [128, GROUP])
        xu = [sb(f"xu{i}", [128, TILES, C]) for i in range(2)]
        std1 = sb("std1", [128, TILES])
        rstd1 = sb("rstd1", [128, TILES])
        y1 = sb("y1", [128, TILES, C])
        st2 = sb("st2", [128, TILES // 2, 6])
        std2 = sb("std2", [128, TILES])
        rstd2 = sb("rstd2", [128, TILES])
        x1 = sb("x1", [128, TILES, C])
        x1T = sb("x1T", [128, GROUP])
        x1b2 = [sb(f"x1b2{i}", [128, TILES, C]) for i in range(2)]
        x1beta = [sb(f"x1beta{i}", [128, TILES, C]) for i in range(2)]
        hT = sb("hT", [128, FCH, GROUP])
        y2 = sb("y2", [128, TILES, C])
        st3 = sb("st3", [128, TILES // 2, 6])
        std3 = sb("std3", [128, TILES])
        rstd3 = sb("rstd3", [128, TILES])
        y2n = sb("y2n", [128, TILES, C])
        y2g = sb("y2g", [128, TILES, C])
        y3 = sb("y3", [128, TILES, C])
        st4 = sb("st4", [128, TILES // 2, 6])
        std4 = sb("std4", [128, TILES])
        rstd4 = sb("rstd4", [128, TILES])
        res = [sb(f"res{i}", [128, TILES, C]) for i in range(2)]

        xT_ps = bank("xT_ps")
        z_ps = bank("z_ps")
        y_ps = bank("y_ps")
        x1T_ps = bank("x1T_ps")
        up_ps = [bank("up_ps0"), bank("up_ps1")]
        down_ps = bank("down_ps")
        prep_ps = bank("prep_ps")
        var_ps = z_ps[:, 0:TILES]

        w_loaded = sem("w_loaded")
        rows_loaded = sem("rows_loaded")
        x_loaded = [sem("x_loaded0"), sem("x_loaded1")]
        res_free = [sem("res_free0"), sem("res_free1")]
        const_set = sem("const_set")
        consts = sem("consts")
        w_turned = sem("w_turned")
        w_ready = sem("w_ready")
        u_done = sem("u_done")
        masks_ready = sem("masks_ready")
        gram_done = sem("gram_done")
        ev_done = sem("ev_done")
        s_done = sem("s_done")
        pt_done = sem("pt_done")
        p_done = sem("p_done")
        xT_done = sem("xT_done")
        z_done = sem("z_done")
        y_done = sem("y_done")
        x1T_done = sem("x1T_done")
        up_done = sem("up_done")
        down_done = sem("down_done")
        G_out = sem("G_out")
        PT_out = sem("PT_out")
        P_out = sem("P_out")
        xT_out = sem("xT_out")
        z_out = sem("z_out")
        std1_out = sem("std1_out")
        std2_out = sem("std2_out")
        std3_out = sem("std3_out")
        std4_out = sem("std4_out")
        x1T_out = sem("x1T_out")
        relu_out = sem("relu_out")
        EV_out = sem("EV_out")
        S_out = sem("S_out")
        r1_out = sem("r1_out")
        y1_out = sem("y1_out")
        st2_out = sem("st2_out")
        r2_out = sem("r2_out")
        x1_out = sem("x1_out")
        y2_out = sem("y2_out")
        st3_out = sem("st3_out")
        r3_out = sem("r3_out")
        y2n_out = sem("y2n_out")
        st4_out = sem("st4_out")
        r4_out = sem("r4_out")
        res_out = sem("res_out")
        xu_out = sem("xu_out")
        sq_out = sem("sq_out")
        m_step = sem("m_step")
        M_out = sem("M_out")
        x1b2_out = sem("x1b2_out")
        x1beta_out = sem("x1beta_out")
        y2g_out = sem("y2g_out")
        y3_out = sem("y3_out")

        def wait(eng, s, value):
            if isinstance(value, int) and value <= 0:
                return
            eng.wait_ge(s, value)

        def two(stats, k):
            return stats[:, :, k:6:3]

        def pairs(t, i):
            return t[:, 2 * i:2 * i + 2, :].rearrange("p t c -> p c t")

        def rows(t, n=TILES):
            return t.unsqueeze(1).to_broadcast([128, n, 128])

        class Step:
            def __init__(self, c, i=None):
                self.c, self.i = c, i
                self.s = c % PERIOD
                self.n = c if i is None else i * PERIOD + c

                def has(k):
                    return i is not None or 0 <= c + k < GROUPS

                self.cur, self.prev, self.nxt, self.nxt2 = has(0), has(-1), has(1), has(2)
                self.prep = c % 2 == 0 and has(2)
                self.gram = c % 2 == 1 and has(3)

            def seq(self, k):
                q = (self.c + k) // SEQ_GROUPS
                return q if self.i is None else self.i * (PERIOD // SEQ_GROUPS) + q

            def slot(self, k):
                return ((self.s + k) // SEQ_GROUPS) % 2

            def loads(self, k):
                q = (self.c + k) // PERIOD + 1
                return 16 * q if self.i is None else (self.i + q) * 16

        def run_steps(eng, body):
            first, loops = 1, (GROUPS - 4) // PERIOD
            for c in range(-2, first):
                body(Step(c))
            with eng.Fori(0, loops) as i:
                for c in range(first, first + PERIOD):
                    body(Step(c, i))
            for c in range(first + loops * PERIOD, GROUPS + 1):
                body(Step(c))

        ROWS = 16 * (5 + 3 + 4 + 4 + 3)

        block = ctx.enter_context(nc.Block())

        @block.sync
        def _(sp):
            def load_x(b, slot):
                sp.dma_start(X[slot][:, :, 0:C], x_v[b, :, :, :]).then_inc(x_loaded[slot], 16)

            for g in range(SEQ_GROUPS):
                sp.sem_inc(res_free[g], 16)
            load_x(0, 0)
            for i, w in enumerate((Wq, Wk1, Wk2, Wv1, Wv2, Wo)):
                sp.dma_start(w_raw[:, i, :], w[:, :]).then_inc(w_loaded, 16)
            load_x(1, 1)

            def pair(b, last):
                for k in range(2):
                    if not last:
                        wait(sp, xu_out, (b + k) * 2 + 2)
                        wait(sp, xT_done, (b + k) * 2 + 2)
                        sp.dma_start(X[k][:, :, 0:C],
                                     x_v[b + (k + 2), :, :, :] if isinstance(b, int) else
                                     x_v[bass.ds(b + (k + 2), 1), :, :, :].rearrange("o p t c -> (o p) t c")
                                     ).then_inc(x_loaded[k], 16)
                    for g in range(SEQ_GROUPS):
                        n = (b + k) * 2 + g
                        wait(sp, res_out, n + 1)
                        o = (out_v[b + k, :, :, :] if isinstance(b, int) else
                             out_v[bass.ds(b + k, 1), :, :, :].rearrange("o p t c -> (o p) t c"))
                        sp.dma_start(o[:, g * TILES:(g + 1) * TILES, :], res[g][:, :, :]).then_inc(res_free[g], 16)

            with sp.Fori(0, BATCHES // 2 - 1) as i:
                pair(i * 2, False)
            pair(BATCHES - 2, True)
            for g in range(SEQ_GROUPS):
                sp.wait_ge(res_free[g], 16 * (BATCHES + 1))

        @block.gpsimd
        def _(pool):
            def columns(dst, v):
                pool.dma_start(dst, v.rearrange("(p o) -> p o", o=1)).then_inc(rows_loaded, 16)

            def spread(dst, v):
                pool.dma_start(dst, v.rearrange("(o c) -> o c", o=1).to_broadcast([128, C])).then_inc(rows_loaded, 16)

            pool.memset(ident[:, :], 0.0).then_inc(const_set, 1)
            pool.memset(head_mask[:, :], 1.0).then_inc(const_set, 1)
            pool.memset(ones[:, :], 1.0)
            pool.memset(center[:, :], -1.0 / C)
            pool.memset(inv_c[:, :], 1.0 / C)
            pool.memset(eps_col[:, :], EPS)
            pool.memset(AqT[:, C + 1:XW], 0.0)
            for i in range(2):
                pool.memset(X[i][:, :, C:C + 1], 1.0)
                pool.memset(X[i][:, :, C + 1:XW], 0.0)
            pool.wait_ge(const_set, 2)
            pool.affine_select(out=ident[:, :], in_=ident[:, :], compare_op=ALU.not_equal, fill=1.0, base=0,
                               pattern=[[-1, 128]], channel_multiplier=1).then_inc(consts, 1)
            columns(cols[:, 0:1], bk1)
            columns(cols[:, 1:2], bk2)
            columns(cols[:, 2:3], ln_g)
            columns(cols[:, 3:4], ln_b)
            columns(AqT[:, C:C + 1], bq)
            for i, v in enumerate((bv1, bv2, bv1)):
                spread(bv_rows[:, i, :], v)
            for i, g in enumerate((g1, g3, g4, g2)):
                pool.dma_start(gcols[:, i:i + 1],
                               g.rearrange("(h o) -> h o", o=1).to_broadcast([HEADS, HEAD])).then_inc(rows_loaded, 16)
            spread(bo_rows[:, :], bo)
            spread(b2_rows[:, :], b2[0, :])
            spread(gamma_rows[:, :], gamma)
            spread(beta_rows[:, :], beta)
            with nc.allow_non_contiguous_dma(reason="b1 by columns, once"):
                pool.dma_start(b1_sb[:, :], b1[0, :].rearrange("(k p) -> p k", p=128)).then_inc(rows_loaded, 16)
            pool.dma_start(w1_sb[:, :], w1[0, :, :]).then_inc(rows_loaded, 16)
            pool.dma_start(w2_sb[:, :, :], w2[0, :, :].rearrange("(k p) c -> p k c", p=128)).then_inc(rows_loaded, 16)

            blocks = head_mask[:, :].rearrange("p (h j) -> p h j", j=HEAD)
            pool.affine_select(out=blocks, in_=blocks, compare_op=ALU.is_ge, fill=0.0, base=0,
                               pattern=[[-HEAD, HEADS], [0, HEAD]], channel_multiplier=1).then_inc(const_set, 1)
            pool.wait_ge(const_set, 3)
            pool.affine_select(out=blocks, in_=blocks, compare_op=ALU.is_ge, fill=0.0, base=HEAD - 1,
                               pattern=[[HEAD, HEADS], [0, HEAD]], channel_multiplier=-1).then_inc(consts, 1)
            pool.wait_ge(consts, 2)
            pool.wait_ge(masks_ready, 1)

            def prepare(b1_):
                wait(pool, S_out, b1_)
                wait(pool, pt_done, b1_ - 1)
                k = (b1_ - 1) * 4
                pool.tensor_tensor(gv[:, :, :], V_sb[:, :, :], gmask[:, 0:2, :], ALU.mult).then_inc(m_step, 1)
                pool.tensor_tensor(S12[:, :], S_sb[:, 0, :], S_sb[:, 1, :], ALU.mult).then_inc(m_step, 1)
                wait(pool, m_step, k + 2)
                pool.tensor_tensor(T_sb[:, :, :], S_sb[:, :, :], gv[:, :, :], ALU.mult).then_inc(m_step, 1)
                pool.tensor_tensor(S12g[:, :, :], rows(S12[:, :], 2), gmask[:, 2:4, :], ALU.mult).then_inc(m_step, 1)
                wait(pool, m_step, k + 4)
                pool.tensor_tensor(M_half[:, :], T_sb[:, 0, :], T_sb[:, 1, :], ALU.add).then_inc(M_out, 1)
                wait(pool, M_out, b1_ * 2 - 1)
                pool.tensor_tensor(M_sb[:, :], M_half[:, :], S12g[:, 0, :], ALU.add).then_inc(M_out, 1)

            def body(st):
                n, s = st.n, st.s
                if st.prev:
                    wait(pool, y2n_out, n)
                    pool.tensor_tensor(y2g[:, :, :], y2n[:, :, :], rows(gamma_rows[:, :]), ALU.mult).then_inc(y2g_out, 1)
                    wait(pool, y2g_out, n)
                    wait(pool, x1beta_out, n)
                    pool.tensor_tensor(y3[:, :, :], y2g[:, :, :], x1beta[(s - 1) % 2][:, :, :], ALU.add).then_inc(y3_out, 1)
                if st.nxt:
                    wait(pool, z_out, n + 2)
                    wait(pool, y_done, n + 1)
                    pool.tensor_tensor(zT_sq[:, :], zT[:, :], zT[:, :], ALU.mult).then_inc(sq_out, 1)
                if st.prep:
                    prepare(st.seq(2) + 1)
                if st.nxt2:
                    m = n + 2
                    slot, g = st.slot(2), s % 2
                    wait(pool, x_loaded[slot], st.loads(2))
                    wait(pool, y1_out, m - 1)
                    pool.tensor_tensor(xu[s % 2][:, :, :], X[slot][:, g * TILES:(g + 1) * TILES, 0:C],
                                       rows(u_rows[:, :]), ALU.add).then_inc(xu_out, 1)
                if st.nxt:
                    m = n + 1
                    wait(pool, x1_out, m + 1)
                    wait(pool, y2_out, m - 1)
                    pool.tensor_tensor(x1b2[(s + 1) % 2][:, :, :], x1[:, :, :], rows(b2_rows[:, :]), ALU.add).then_inc(x1b2_out, 1)
                    wait(pool, y3_out, m - 1)
                    pool.tensor_tensor(x1beta[(s + 1) % 2][:, :, :], x1[:, :, :], rows(beta_rows[:, :]), ALU.add).then_inc(x1beta_out, 1)

            run_steps(pool, body)

        @block.scalar
        def _(act):
            def turned(k, dst, src):
                act.wait_ge(w_turned, k)
                act.activation(dst, src, ACT.Copy).then_inc(w_ready, 1)

            turned(1, Ak[:, 0, :], y_ps[:, 0:128])
            turned(2, Ak[:, 1, :], x1T_ps[:, 0:128])
            turned(3, Av[:, 0, :], up_ps[0][:, 0:128])
            turned(4, Av[:, 1, :], up_ps[1][:, 0:128])
            turned(5, WoT[:, :], down_ps[:, 0:128])
            act.wait_ge(consts, 1)
            act.wait_ge(rows_loaded, ROWS)
            act.activation(lnb_wide[:, :], ones[:, :], ACT.Copy, scale=cols[:, 3:4]).then_inc(w_ready, 1)
            act.wait_ge(w_ready, 5)
            act.activation(Wog[:, :], WoT[:, :], ACT.Copy, scale=cols[:, 2:3]).then_inc(w_ready, 1)

            def std(src, dst, done, scale):
                act.activation(dst[:, :], src, ACT.Sqrt, bias=eps_col[:, :], scale=scale).then_inc(done, 1)

            def relu(st, k):
                n = st.n
                wait(act, up_done, n * FCH + (k + 1))
                act.activation(hT[:, k, :], up_ps[k % 2][:, :], ACT.Relu, bias=b1_sb[:, k:k + 1]).then_inc(relu_out, 1)

            def body(st):
                n, s = st.n, st.s
                if st.c == -2:
                    act.wait_ge(gram_done, 1)
                    act.activation(G_sb[:, :], prep_ps[:, 0:XW], ACT.Copy).then_inc(G_out, 1)
                if st.cur:
                    relu(st, 0)
                if st.prev:
                    wait(act, st3_out, n)
                    std(two(st3, 2), std3, std3_out, 1.0 / C)
                if st.cur:
                    relu(st, 1)
                if st.nxt:
                    m = n + 1
                    wait(act, z_done, m + 1)
                    wait(act, y_done, m)
                    wait(act, sq_out, m)
                    act.activation(zT[:, :], z_ps[:, :], ACT.Identity, bias=P_sb[:, C:C + 1]).then_inc(z_out, 1)
                if st.cur:
                    relu(st, 2)
                    relu(st, 3)
                if st.nxt:
                    wait(act, y_done, n + 2)
                    wait(act, r1_out, n + 1)
                    std(var_ps, std1, std1_out, 1.0)
                if st.nxt:
                    wait(act, st2_out, n + 2)
                    wait(act, r2_out, n + 1)
                    std(two(st2, 2), std2, std2_out, 1.0 / C)
                if st.prev:
                    wait(act, st4_out, n)
                    std(two(st4, 2), std4, std4_out, 1.0 / C)
                if st.prep:
                    b = st.seq(2)
                    wait(act, pt_done, b + 1)
                    wait(act, p_done, b)
                    act.activation(PT_sb[:, :], prep_ps[:, 0:XW], ACT.Copy).then_inc(PT_out, 1)
                    wait(act, p_done, b + 1)
                    wait(act, z_done, b * 2)
                    act.activation(P_sb[:, 0:C + 1], prep_ps[:, 0:C + 1], ACT.Copy).then_inc(P_out, 1)
                if st.nxt2:
                    m = n + 2
                    wait(act, xT_done, m + 1)
                    wait(act, z_done, m)
                    act.activation(xT[:, :], xT_ps[:, :], ACT.Copy).then_inc(xT_out, 1)
                if st.nxt:
                    m = n + 1
                    wait(act, x1T_done, m + 1)
                    wait(act, up_done, m * FCH)
                    act.activation(x1T[:, :], x1T_ps[:, :], ACT.Copy).then_inc(x1T_out, 1)
                if st.gram:
                    b = st.seq(3)
                    wait(act, gram_done, b + 1)
                    wait(act, ev_done, b)
                    wait(act, EV_out, b)
                    act.activation(G_sb[:, :], prep_ps[:, 0:XW], ACT.Copy).then_inc(G_out, 1)

            run_steps(act, body)

        @block.vector
        def _(dve):
            dve.wait_ge(consts, 1)
            dve.wait_ge(w_loaded, 16 * 6)
            dve.wait_ge(rows_loaded, ROWS)
            dve.tensor_tensor(AqT[:, 0:C], w_raw[:, 0, :], ident[:, :], ALU.add)
            dve.tensor_tensor(center[:, :], center[:, :], ident[:, :], ALU.add)
            dve.tensor_scalar(nbv_rows[:, :, :], bv_rows[:, 1:3, :], float(SEQ), None, ALU.mult)
            dve.wait_ge(consts, 2)
            for i in range(4):
                dve.tensor_scalar(gmask[:, i, :], head_mask[:, :], gcols[:, i:i + 1], 1.0 / (SEQ * SEQ), ALU.mult, ALU.mult)
            dve.wait_ge(w_ready, 4)
            for i in range(2):
                dve.tensor_tensor(Ak[:, i, :], Ak[:, i, :], ident[:, :], ALU.add)
            dve.tensor_tensor(Av[:, 2, :], Av[:, 0, :], ident[:, :], ALU.add)
            dve.tensor_tensor(Av[:, 1, :], Av[:, 1, :], ident[:, :], ALU.add)
            dve.tensor_tensor(Av[:, 0, :], Av[:, 0, :], ident[:, :], ALU.add)
            dve.wait_ge(u_done, 1)
            dve.tensor_tensor(u_rows[:, :], xT_ps[:, 0:C], bo_rows[:, :], ALU.add).then_inc(masks_ready, 1)

            def stats(t, st, done):
                for i in range(TILES // 2):
                    last = dve.bn_stats(st[:, i, :], pairs(t, i))
                last.then_inc(done, 1)

            def normalize(dst, src, st, rstd, done):
                for t in range(TILES):
                    last = dve.tensor_scalar(dst[:, t, :], src[:, t, :], st[:, t // 2, 3 * (t % 2) + 1:3 * (t % 2) + 2],
                                             rstd[:, t:t + 1], ALU.subtract, ALU.mult)
                last.then_inc(done, 1)

            def body(st):
                n, s = st.n, st.s
                if st.prev:
                    wait(dve, down_done, n)
                    wait(dve, x1b2_out, n)
                    dve.tensor_tensor(y2[:, :, :], down_ps[:, :].rearrange("p (t c) -> p t c", c=C),
                                      x1b2[(s - 1) % 2][:, :, :], ALU.add).then_inc(y2_out, 1)
                    wait(dve, y2_out, n)
                    stats(y2, st3, st3_out)
                if st.prep:
                    b = st.seq(2)
                    wait(dve, ev_done, b + 1)
                    wait(dve, s_done, b)
                    wait(dve, M_out, b * 2)
                    dve.scalar_tensor_tensor(out=E_sb[:, :, :].rearrange("p j c -> p (j c)"),
                                             in0=bv_rows[:, 0:2, :].rearrange("p j c -> p (j c)"),
                                             scalar=G_sb[:, C:C + 1], in1=prep_ps[:, 0:256],
                                             op0=ALU.mult, op1=ALU.add)
                    dve.tensor_tensor(V_sb[:, :, :].rearrange("p j c -> p (j c)"), prep_ps[:, 256:512],
                                      nbv_rows[:, :, :].rearrange("p j c -> p (j c)"), ALU.add).then_inc(EV_out, 1)
                if st.prev:
                    wait(dve, std3_out, n)
                    dve.reciprocal(rstd3[:, :], std3[:, :]).then_inc(r3_out, 1)
                    wait(dve, r3_out, n)
                    normalize(y2n, y2, st3, rstd3, y2n_out)
                if st.prep:
                    b = st.seq(2)
                    wait(dve, EV_out, b + 1)
                    wait(dve, s_done, b + 1)
                    for j in range(2):
                        last = dve.scalar_tensor_tensor(out=S_sb[:, j, :], in0=V_sb[:, 1 - j, :],
                                                        scalar=cols[:, j:j + 1],
                                                        in1=prep_ps[:, j * 128:(j + 1) * 128],
                                                        op0=ALU.mult, op1=ALU.add)
                    last.then_inc(S_out, 1)
                if st.nxt:
                    m = n + 1
                    wait(dve, std1_out, m + 1)
                    dve.reciprocal(rstd1[:, :], std1[:, :]).then_inc(r1_out, 1)
                    wait(dve, r1_out, m + 1)
                    wait(dve, y_done, m + 1)
                    wait(dve, xu_out, m + 1)
                    for t in range(TILES):
                        last = dve.scalar_tensor_tensor(out=y1[:, t, :], in0=y_ps[:, t * C:(t + 1) * C],
                                                        scalar=rstd1[:, t:t + 1], in1=xu[(s + 1) % 2][:, t, :],
                                                        op0=ALU.mult, op1=ALU.add)
                    last.then_inc(y1_out, 1)
                    wait(dve, y1_out, m + 1)
                    stats(y1, st2, st2_out)
                if st.prev:
                    wait(dve, y3_out, n)
                    stats(y3, st4, st4_out)
                if st.nxt:
                    m = n + 1
                    wait(dve, std2_out, m + 1)
                    dve.reciprocal(rstd2[:, :], std2[:, :]).then_inc(r2_out, 1)
                    wait(dve, r2_out, m + 1)
                    wait(dve, x1T_done, m)
                    wait(dve, x1beta_out, m)
                    normalize(x1, y1, st2, rstd2, x1_out)
                if st.prev:
                    wait(dve, std4_out, n)
                    dve.reciprocal(rstd4[:, :], std4[:, :]).then_inc(r4_out, 1)
                    wait(dve, r4_out, n)
                    wait(dve, res_free[(s - 1) % 2], st.seq(-1) * 16 + 16)
                    normalize(res[(s - 1) % 2], y3, st4, rstd4, res_out)

            run_steps(dve, body)

        @block.tensor
        def _(pe):
            def mm(o, lhsT, rhs, start=True, stop=True, **kw):
                return pe.matmul(o, lhsT, rhs, start=start, stop=stop, **kw)

            pe.wait_ge(consts, 1)
            pe.wait_ge(w_loaded, 16 * 6)
            for i, dst in ((1, y_ps), (2, x1T_ps), (3, up_ps[0]), (4, up_ps[1]), (5, down_ps)):
                pe.transpose(dst[:, 0:128], w_raw[:, i, :], ident[:, :]).then_inc(w_turned, 1)
            pe.wait_ge(w_ready, 7)
            mm(xT_ps[:, 0:C], lnb_wide[:, :], WoT[:, :]).then_inc(u_done, 1)

            def gram(b1_, m, slot):
                wait(pe, x_loaded[slot], m)
                wait(pe, P_out, b1_ - 1)
                for t in range(SEQ_TILES):
                    last = mm(prep_ps[:, 0:XW], X[slot][:, t, 0:C], X[slot][:, t, :],
                              start=(t == 0), stop=(t == SEQ_TILES - 1))
                last.then_inc(gram_done, 1)

            def up(n, k):
                wait(pe, x1T_out, n + 1)
                wait(pe, relu_out, n * FCH + (k - 1))
                mm(up_ps[k % 2][:, :], w1_sb[:, k * 128:(k + 1) * 128], x1T[:, :]).then_inc(up_done, 1)

            def body(st):
                n, s = st.n, st.s
                if st.c == -2:
                    pe.wait_ge(masks_ready, 1)
                    gram(1, 16, 0)
                if st.cur:
                    up(n, 0)
                    up(n, 1)
                if st.prep:
                    b = st.seq(2)
                    wait(pe, G_out, b + 1)
                    mm(prep_ps[:, 0:256], G_sb[:, 0:C], Av[:, 0:2, :].rearrange("p j c -> p (j c)"))
                    mm(prep_ps[:, 256:512], G_sb[:, C:C + 1].to_broadcast([128, 128]),
                       Av[:, 1:3, :].rearrange("p j c -> p (j c)")).then_inc(ev_done, 1)
                if st.nxt:
                    m = n + 1
                    wait(pe, xT_out, m + 1)
                    wait(pe, P_out, st.seq(1) + 1)
                    wait(pe, std1_out, m)
                    mm(z_ps[:, :], P_sb[:, 0:C], xT[:, :]).then_inc(z_done, 1)
                if st.cur:
                    up(n, 2)
                    up(n, 3)
                if st.prep:
                    b = st.seq(2)
                    wait(pe, EV_out, b + 1)
                    for j in range(2):
                        last = mm(prep_ps[:, j * 128:(j + 1) * 128], Ak[:, j, :], E_sb[:, j, :])
                    last.then_inc(s_done, 1)
                if st.nxt:
                    m = n + 1
                    wait(pe, z_out, m + 1)
                    wait(pe, y1_out, m)
                    for t in range(TILES):
                        mm(y_ps[:, t * C:(t + 1) * C], zT[:, t * TILE:(t + 1) * TILE], Wog[:, :])
                    wait(pe, sq_out, m + 1)
                    for t in range(TILES):
                        last = mm(z_ps[:, t:t + 1], zT_sq[:, t * TILE:(t + 1) * TILE], inv_c[:, :])
                    last.then_inc(y_done, 1)
                if st.cur:
                    wait(pe, relu_out, n * FCH + FCH)
                    wait(pe, y2_out, n)
                    for t in range(TILES):
                        if t == 2 and st.prep:
                            pt(st.seq(2))
                        for k in range(FCH):
                            last = mm(down_ps[:, t * C:(t + 1) * C], hT[:, k, t * TILE:(t + 1) * TILE], w2_sb[:, k, :],
                                      start=(k == 0), stop=(k == FCH - 1))
                    last.then_inc(down_done, 1)
                elif st.prep:
                    pt(st.seq(2))
                if st.prep:
                    b = st.seq(2)
                    wait(pe, PT_out, b + 1)
                    mm(prep_ps[:, 0:C], PT_sb[:, 0:C], center[:, :])
                    mm(prep_ps[:, C:C + 1], center[:, :], PT_sb[:, C:C + 1]).then_inc(p_done, 1)
                if st.nxt2:
                    m = n + 2
                    slot, g = st.slot(2), s % 2
                    wait(pe, x_loaded[slot], st.loads(2))
                    wait(pe, xT_out, m)
                    for t in range(TILES):
                        last = pe.transpose(xT_ps[:, t * TILE:(t + 1) * TILE], X[slot][:, g * TILES + t, 0:C], ident[:, :])
                    last.then_inc(xT_done, 1)
                if st.nxt:
                    m = n + 1
                    wait(pe, x1_out, m + 1)
                    wait(pe, x1T_out, m)
                    for t in range(TILES):
                        last = pe.transpose(x1T_ps[:, t * TILE:(t + 1) * TILE], x1[:, t, :], ident[:, :])
                    last.then_inc(x1T_done, 1)
                if st.gram:
                    b = st.seq(3)
                    slot = st.slot(3)
                    gram(b + 1, st.loads(3), slot)

            def pt(b):
                wait(pe, M_out, (b + 1) * 2)
                mm(prep_ps[:, 0:XW], M_sb[:, :], AqT[:, :], start=True, stop=False)
                mm(prep_ps[:, C:C + 1], S12g[:, 1, :], ones[:, 0:1], start=False, stop=True).then_inc(pt_done, 1)

            run_steps(pe, body)


_ATTN = ['x', 'Wq', 'bq', 'Wk1', 'bk1', 'Wk2', 'bk2', 'Wv1', 'bv1', 'Wv2', 'bv2', 'g1', 'g2', 'g3', 'g4',
         'ln_g', 'ln_b', 'Wo', 'bo']
_FFN = ['w1', 'b1', 'w2', 'b2', 'gamma', 'beta']
_INS = ['L0_attn_' + n for n in _ATTN] + ['L0_ffn_' + n for n in _FFN]


def kernel(**inputs):
    import numpy as _np
    import concourse.bacc as _bacc
    from concourse import mybir as _mybir
    from concourse.bass_utils import run_bass_kernel_spmd as _run

    nc = _bacc.Bacc("TRN2", target_bir_lowering=False, num_devices=1)
    arrays, args = {}, []
    for name in _INS:
        a = _np.ascontiguousarray(inputs[name])
        arrays[f"in_{name}"] = a
        args.append(nc.dram_tensor(f"in_{name}", a.shape, _mybir.dt.from_np(a.dtype), kind="ExternalInput").ap())
    out = nc.dram_tensor("out_0", (BATCHES, SEQ, C), _mybir.dt.float32, kind="ExternalOutput").ap()
    build(nc, *args, out)
    r = _run(nc, [arrays], core_ids=[0])
    return r.results[0]["out_0"]
```

```python
from contextlib import ExitStack

import concourse.bass as bass
from concourse import mybir

BATCHES, SEQ, C, HEADS, FF = 8, 1024, 128, 16, 512
HEAD = C // HEADS
EPS = 1e-5
TILE = 128
SEQ_TILES = SEQ // TILE
TILES = 4
GROUP = TILES * TILE
SEQ_GROUPS = SEQ // GROUP
GROUPS = BATCHES * SEQ_GROUPS
FCH = FF // 128
XW = C + 2
PERIOD = 4


def build(nc, x, Wq, bq, Wk1, bk1, Wk2, bk2, Wv1, bv1, Wv2, bv2, g1, g2, g3, g4, ln_g, ln_b, Wo, bo,
          w1, b1, w2, b2, gamma, beta, out):
    f32 = mybir.dt.float32
    f32r = mybir.dt.float32r
    ALU = mybir.AluOpType
    ACT = mybir.ActivationFunctionType

    x_v = x.rearrange("b (p t) c -> b p t c", t=SEQ_TILES)
    out_v = out.rearrange("b (p t) c -> b p t c", t=SEQ_TILES)

    ctx = ExitStack()
    with ctx:
        def sb(name, shape, dt=f32):
            return ctx.enter_context(nc.sbuf_tensor(name, shape, dt))

        def bank(name):
            return ctx.enter_context(nc.psum_tensor(name, [128, 512], f32))

        def sem(name):
            return ctx.enter_context(nc.semaphore(name))

        ident = sb("ident", [128, 128])
        ones = sb("ones", [128, 128])
        center = sb("center", [128, 128])
        inv_c = sb("inv_c", [128, 1])
        head_mask = sb("head_mask", [128, 128])
        w_raw = sb("w_raw", [128, 6, 128])
        AqT = sb("AqT", [128, XW])
        A_kv = sb("A_kv", [128, 5, 128])
        WoT = sb("WoT", [128, 128])
        Wog = sb("Wog", [128, 128])
        bv_rows = sb("bv_rows", [128, 3, 128])
        nbv_rows = sb("nbv_rows", [128, 2, 128])
        cols = sb("cols", [128, 4])
        gcols = sb("gcols", [128, 4])
        gmask = sb("gmask", [128, 4, 128])
        lnb_wide = sb("lnb_wide", [128, 128])
        bo_rows = sb("bo_rows", [128, 128])
        u_rows = sb("u_rows", [128, 128])
        w1_sb = sb("w1_sb", [128, FF])
        w1_hi = sb("w1_hi", [128, FF], f32r)
        w1_lo = sb("w1_lo", [128, FF], f32r)
        b1_sb = sb("b1_sb", [128, FCH])
        w2_sb = sb("w2_sb", [128, FCH, C])
        b2_rows = sb("b2_rows", [128, C])
        gamma_rows = sb("gamma_rows", [128, C])
        beta_rows = sb("beta_rows", [128, C])
        eps_col = sb("eps_col", [128, 1])
        warm = sb("warm", [128, 1])

        X = [sb(f"X{i}", [128, SEQ_TILES, XW]) for i in range(2)]
        G_sb = sb("G_sb", [128, XW])
        E_sb = sb("E_sb", [128, 2, 128])
        V_sb = sb("V_sb", [128, 2, 128])
        S_sb = sb("S_sb", [128, 2, 128])
        gv = sb("gv", [128, 2, 128])
        T_sb = sb("T_sb", [128, 2, 128])
        S12 = sb("S12", [128, 128])
        S12g = sb("S12g", [128, 2, 128])
        M_half = sb("M_half", [128, 128])
        M_sb = sb("M_sb", [128, 128])
        PT_sb = sb("PT_sb", [128, XW])
        P_sb = sb("P_sb", [128, XW])

        xT = sb("xT", [128, GROUP])
        zT = sb("zT", [128, GROUP])
        zT_sq = sb("zT_sq", [128, GROUP])
        xu = [sb(f"xu{i}", [128, TILES, C]) for i in range(2)]
        std1 = sb("std1", [128, TILES])
        rstd1 = sb("rstd1", [128, TILES])
        y1 = sb("y1", [128, TILES, C])
        st2 = sb("st2", [128, TILES // 2, 6])
        std2 = sb("std2", [128, TILES])
        rstd2 = sb("rstd2", [128, TILES])
        x1 = sb("x1", [128, TILES, C])
        x1T_hi = sb("x1T_hi", [128, GROUP], f32r)
        x1T_lo = sb("x1T_lo", [128, GROUP], f32r)
        x1b2 = [sb(f"x1b2{i}", [128, TILES, C]) for i in range(2)]
        x1beta = [sb(f"x1beta{i}", [128, TILES, C]) for i in range(2)]
        hT = sb("hT", [128, FCH, GROUP])
        y2 = sb("y2", [128, TILES, C])
        st3 = sb("st3", [128, TILES // 2, 6])
        std3 = sb("std3", [128, TILES])
        rstd3 = sb("rstd3", [128, TILES])
        y2n = sb("y2n", [128, TILES, C])
        y2g = sb("y2g", [128, TILES, C])
        y3 = sb("y3", [128, TILES, C])
        st4 = sb("st4", [128, TILES // 2, 6])
        std4 = sb("std4", [128, TILES])
        rstd4 = sb("rstd4", [128, TILES])
        res = [sb(f"res{i}", [128, TILES, C]) for i in range(2)]

        turn_ps = bank("turn_ps")
        z_ps = bank("z_ps")
        y_ps = bank("y_ps")
        up_ps = [bank("up_ps0"), bank("up_ps1"), bank("up_ps2")]
        down_ps = bank("down_ps")
        prep_ps = bank("prep_ps")
        var_ps = z_ps[:, 0:TILES]
        kv_ps = turn_ps[:, :].rearrange("p (j c) -> p j c", c=128)

        kv_loaded = sem("kv_loaded")
        bv_loaded = sem("bv_loaded")
        bk_loaded = sem("bk_loaded")
        ln_loaded = sem("ln_loaded")
        qo_loaded = sem("qo_loaded")
        attn_rows = sem("attn_rows")
        ffn_rows = sem("ffn_rows")
        x_loaded = [sem("x_loaded0"), sem("x_loaded1")]
        res_free = [sem("res_free0"), sem("res_free1")]
        const_set = sem("const_set")
        consts = sem("consts")
        kv_turned = sem("kv_turned")
        o_turned = sem("o_turned")
        lnb_ready = sem("lnb_ready")
        WoT_ready = sem("WoT_ready")
        A_ready = sem("A_ready")
        nbv_ready = sem("nbv_ready")
        u_done = sem("u_done")
        masks_ready = sem("masks_ready")
        u_ready = sem("u_ready")
        gram_done = sem("gram_done")
        ev_done = sem("ev_done")
        s_done = sem("s_done")
        pt_done = sem("pt_done")
        p_done = sem("p_done")
        xT_done = sem("xT_done")
        z_done = sem("z_done")
        var_done = sem("var_done")
        y_done = sem("y_done")
        x1T_done = sem("x1T_done")
        up_done = sem("up_done")
        down_done = sem("down_done")
        G_out = sem("G_out")
        PT_out = sem("PT_out")
        P_out = sem("P_out")
        xT_out = sem("xT_out")
        z_out = sem("z_out")
        std1_out = sem("std1_out")
        std2_out = sem("std2_out")
        std3_out = sem("std3_out")
        std4_out = sem("std4_out")
        x1hi_out = sem("x1hi_out")
        relu_out = sem("relu_out")
        EV_out = sem("EV_out")
        S_out = sem("S_out")
        w1_split = sem("w1_split")
        x1lo_out = sem("x1lo_out")
        r1_out = sem("r1_out")
        y1_out = sem("y1_out")
        st2_out = sem("st2_out")
        r2_out = sem("r2_out")
        x1_out = sem("x1_out")
        y2_out = sem("y2_out")
        st3_out = sem("st3_out")
        r3_out = sem("r3_out")
        y2n_out = sem("y2n_out")
        st4_out = sem("st4_out")
        r4_out = sem("r4_out")
        res_out = sem("res_out")
        xu_out = sem("xu_out")
        sq_out = sem("sq_out")
        m_step = sem("m_step")
        M_out = sem("M_out")
        x1b2_out = sem("x1b2_out")
        x1beta_out = sem("x1beta_out")
        y2g_out = sem("y2g_out")
        y3_out = sem("y3_out")

        def wait(eng, s, value):
            if isinstance(value, int) and value <= 0:
                return
            eng.wait_ge(s, value)

        def two(stats, k):
            return stats[:, :, k:6:3]

        def pairs(t, i):
            return t[:, 2 * i:2 * i + 2, :].rearrange("p t c -> p c t")

        def column(v):
            return v.rearrange("(p o) -> p o", o=1)

        def spread(v):
            return v.rearrange("(o c) -> o c", o=1).to_broadcast([128, C])

        def rows(t, n=TILES):
            return t.unsqueeze(1).to_broadcast([128, n, 128])

        def prepare(eng, b1_):
            wait(eng, S_out, b1_)
            wait(eng, pt_done, b1_ - 1)
            k = (b1_ - 1) * 4
            eng.tensor_tensor(gv[:, :, :], V_sb[:, :, :], gmask[:, 0:2, :], ALU.mult).then_inc(m_step, 1)
            eng.tensor_tensor(S12[:, :], S_sb[:, 0, :], S_sb[:, 1, :], ALU.mult).then_inc(m_step, 1)
            wait(eng, m_step, k + 2)
            eng.tensor_tensor(T_sb[:, :, :], S_sb[:, :, :], gv[:, :, :], ALU.mult).then_inc(m_step, 1)
            eng.tensor_tensor(S12g[:, :, :], rows(S12[:, :], 2), gmask[:, 2:4, :], ALU.mult).then_inc(m_step, 1)
            wait(eng, m_step, k + 4)
            eng.tensor_tensor(M_half[:, :], T_sb[:, 0, :], T_sb[:, 1, :], ALU.add).then_inc(M_out, 1)
            wait(eng, M_out, b1_ * 2 - 1)
            eng.tensor_tensor(M_sb[:, :], M_half[:, :], S12g[:, 0, :], ALU.add).then_inc(M_out, 1)

        class Step:
            def __init__(self, c, i=None):
                self.c, self.i = c, i
                self.s = c % PERIOD
                self.n = c if i is None else i * PERIOD + c

                def has(k):
                    return i is not None or 0 <= c + k < GROUPS

                self.cur, self.prev, self.prev2 = has(0), has(-1), has(-2)
                self.nxt, self.nxt2 = has(1), has(2)
                self.prep = c % 2 == 0 and has(2)
                self.gram = c % 2 == 1 and has(3)

            def seq(self, k):
                q = (self.c + k) // SEQ_GROUPS
                return q if self.i is None else self.i * (PERIOD // SEQ_GROUPS) + q

            def slot(self, k):
                return ((self.s + k) // SEQ_GROUPS) % 2

            def loads(self, k):
                q = (self.c + k) // PERIOD + 1
                return 16 * q if self.i is None else (self.i + q) * 16

        def run_steps(eng, body):
            first, loops = 2, (GROUPS - 5) // PERIOD
            for c in range(-2, first):
                body(Step(c))
            with eng.Fori(0, loops) as i:
                for c in range(first, first + PERIOD):
                    body(Step(c, i))
            for c in range(first + loops * PERIOD, GROUPS + 2):
                body(Step(c))

        ATTN_ROWS = 16 * (4 + 1)
        FFN_ROWS = 16 * 6

        block = ctx.enter_context(nc.Block())

        @block.sync
        def _(sp):
            def load_x(b, slot):
                sp.dma_start(X[slot][:, :, 0:C], x_v[b, :, :, :]).then_inc(x_loaded[slot], 16)

            for g in range(SEQ_GROUPS):
                sp.sem_inc(res_free[g], 16)
            load_x(0, 0)
            for i, w in enumerate((Wv1, Wv2, Wk1, Wk2)):
                sp.dma_start(w_raw[:, i, :], w[:, :]).then_inc(kv_loaded, 16)
            for i, v in enumerate((bv1, bv2, bv1)):
                sp.dma_start(bv_rows[:, i, :], spread(v)).then_inc(bv_loaded, 16)
            for dst, v in ((cols[:, 0:1], bk1), (cols[:, 1:2], bk2)):
                sp.dma_start(dst, column(v)).then_inc(bk_loaded, 16)
            for i, w in enumerate((Wo, Wq)):
                sp.dma_start(w_raw[:, 4 + i, :], w[:, :]).then_inc(qo_loaded, 16)
            load_x(1, 1)

            def pair(b, last):
                for k in range(2):
                    if not last:
                        wait(sp, xu_out, (b + k) * 2 + 2)
                        wait(sp, xT_done, (b + k) * 2 + 2)
                        sp.dma_start(X[k][:, :, 0:C],
                                     x_v[b + (k + 2), :, :, :] if isinstance(b, int) else
                                     x_v[bass.ds(b + (k + 2), 1), :, :, :].rearrange("o p t c -> (o p) t c")
                                     ).then_inc(x_loaded[k], 16)
                    for g in range(SEQ_GROUPS):
                        n = (b + k) * 2 + g
                        wait(sp, res_out, n + 1)
                        o = (out_v[b + k, :, :, :] if isinstance(b, int) else
                             out_v[bass.ds(b + k, 1), :, :, :].rearrange("o p t c -> (o p) t c"))
                        sp.dma_start(o[:, g * TILES:(g + 1) * TILES, :], res[g][:, :, :]).then_inc(res_free[g], 16)

            with sp.Fori(0, BATCHES // 2 - 1) as i:
                pair(i * 2, False)
            pair(BATCHES - 2, True)
            for g in range(SEQ_GROUPS):
                sp.wait_ge(res_free[g], 16 * (BATCHES + 1))

        @block.gpsimd
        def _(pool):
            pool.memset(ident[:, :], 0.0).then_inc(const_set, 1)
            pool.memset(head_mask[:, :], 1.0).then_inc(const_set, 1)
            pool.wait_ge(const_set, 1)
            pool.affine_select(out=ident[:, :], in_=ident[:, :], compare_op=ALU.not_equal, fill=1.0, base=0,
                               pattern=[[-1, 128]], channel_multiplier=1).then_inc(consts, 1)
            for i in range(2):
                pool.memset(X[i][:, :, C:C + 1], 1.0)
                pool.memset(X[i][:, :, C + 1:XW], 0.0)
            pool.memset(ones[:, :], 1.0)
            pool.memset(center[:, :], -1.0 / C)
            pool.memset(inv_c[:, :], 1.0 / C)
            pool.memset(eps_col[:, :], EPS)
            pool.memset(AqT[:, C + 1:XW], 0.0).then_inc(consts, 1)
            pool.wait_ge(const_set, 2)
            blocks = head_mask[:, :].rearrange("p (h j) -> p h j", j=HEAD)
            pool.affine_select(out=blocks, in_=blocks, compare_op=ALU.is_ge, fill=0.0, base=0,
                               pattern=[[-HEAD, HEADS], [0, HEAD]], channel_multiplier=1).then_inc(const_set, 1)
            pool.wait_ge(const_set, 3)
            pool.affine_select(out=blocks, in_=blocks, compare_op=ALU.is_ge, fill=0.0, base=HEAD - 1,
                               pattern=[[HEAD, HEADS], [0, HEAD]], channel_multiplier=-1).then_inc(consts, 1)
            for i, g in enumerate((g1, g3, g4, g2)):
                pool.dma_start(gcols[:, i:i + 1],
                               g.rearrange("(h o) -> h o", o=1).to_broadcast([HEADS, HEAD])).then_inc(attn_rows, 16)
            pool.dma_start(AqT[:, C:C + 1], column(bq)).then_inc(attn_rows, 16)
            for dst, v in ((b2_rows, b2[0, :]), (beta_rows, beta), (gamma_rows, gamma)):
                pool.dma_start(dst[:, :], spread(v)).then_inc(ffn_rows, 16)
            pool.dma_start(w1_sb[:, :], w1[0, :, :]).then_inc(ffn_rows, 16)
            with nc.allow_non_contiguous_dma(reason="b1 by columns, once"):
                pool.dma_start(b1_sb[:, :], b1[0, :].rearrange("(k p) -> p k", p=128)).then_inc(ffn_rows, 16)
            pool.dma_start(w2_sb[:, :, :], w2[0, :, :].rearrange("(k p) c -> p k c", p=128)).then_inc(ffn_rows, 16)
            pool.wait_ge(masks_ready, 1)

            def body(st):
                n, s = st.n, st.s
                if st.prep and st.c != -2:
                    prepare(pool, st.seq(2) + 1)
                if st.prev and st.c != GROUPS:
                    wait(pool, y2n_out, n)
                    pool.tensor_tensor(y2g[:, :, :], y2n[:, :, :], rows(gamma_rows[:, :]), ALU.mult).then_inc(y2g_out, 1)
                    wait(pool, y2g_out, n)
                    wait(pool, x1beta_out, n)
                    wait(pool, res_out, n - 1)
                    pool.tensor_tensor(y3[:, :, :], y2g[:, :, :], x1beta[(s - 1) % 2][:, :, :], ALU.add).then_inc(y3_out, 1)
                if st.nxt2:
                    m = n + 2
                    slot, g = st.slot(2), s % 2
                    wait(pool, x_loaded[slot], st.loads(2))
                    if st.c == -2:
                        pool.wait_ge(u_ready, 1)
                    wait(pool, y1_out, m - 1)
                    pool.tensor_tensor(xu[s % 2][:, :, :], X[slot][:, g * TILES:(g + 1) * TILES, 0:C],
                                       rows(u_rows[:, :]), ALU.add).then_inc(xu_out, 1)
                if st.nxt:
                    m = n + 1
                    wait(pool, x1_out, m + 1)
                    if st.c == -1:
                        pool.wait_ge(ffn_rows, FFN_ROWS)
                    wait(pool, y2_out, m - 1)
                    pool.tensor_tensor(x1b2[(s + 1) % 2][:, :, :], x1[:, :, :], rows(b2_rows[:, :]), ALU.add).then_inc(x1b2_out, 1)
                    wait(pool, y3_out, m - 1)
                    pool.tensor_tensor(x1beta[(s + 1) % 2][:, :, :], x1[:, :, :], rows(beta_rows[:, :]), ALU.add).then_inc(x1beta_out, 1)

            run_steps(pool, body)

        @block.scalar
        def _(act):
            for dst, v in ((cols[:, 2:3], column(ln_g)), (cols[:, 3:4], column(ln_b)), (bo_rows[:, :], spread(bo))):
                act.dma_start(dst, v).then_inc(ln_loaded, 16)
            act.wait_ge(consts, 2)
            act.activation(warm[:, :], eps_col[:, :], ACT.Sqrt)

            def output_weights():
                act.wait_ge(consts, 2)
                act.wait_ge(ln_loaded, 16 * 3)
                act.activation(lnb_wide[:, :], ones[:, :], ACT.Copy, scale=cols[:, 3:4]).then_inc(lnb_ready, 1)
                act.wait_ge(o_turned, 1)
                act.activation(WoT[:, :], down_ps[:, 0:128], ACT.Copy).then_inc(WoT_ready, 1)
                act.activation(Wog[:, :], down_ps[:, 0:128], ACT.Copy, scale=cols[:, 2:3]).then_inc(WoT_ready, 1)

            def std(src, dst, done, scale):
                act.activation(dst[:, :], src, ACT.Sqrt, bias=eps_col[:, :], scale=scale).then_inc(done, 1)

            def relu(st, k):
                n = st.n
                wait(act, up_done, n * FCH + (k + 1))
                act.activation(hT[:, k, :], up_ps[k % 3][:, :], ACT.Relu, bias=b1_sb[:, k:k + 1]).then_inc(relu_out, 1)

            def body(st):
                n, s = st.n, st.s
                if st.c == -2:
                    act.wait_ge(gram_done, 1)
                    act.activation(G_sb[:, :], prep_ps[:, 0:XW], ACT.Copy).then_inc(G_out, 1)
                    output_weights()
                if st.nxt:
                    m = n + 1
                    wait(act, z_done, m + 1)
                    wait(act, var_done, m)
                    act.activation(zT_sq[:, :], z_ps[:, :], ACT.Square, bias=P_sb[:, C:C + 1]).then_inc(sq_out, 1)
                    wait(act, y_done, m)
                    act.activation(zT[:, :], z_ps[:, :], ACT.Identity, bias=P_sb[:, C:C + 1]).then_inc(z_out, 1)
                if st.cur:
                    if st.c == 0:
                        act.wait_ge(ffn_rows, FFN_ROWS)
                    relu(st, 0)
                if st.prev:
                    wait(act, st3_out, n)
                    std(two(st3, 2), std3, std3_out, 1.0 / C)
                if st.cur:
                    relu(st, 1)
                    relu(st, 2)
                    relu(st, 3)
                if st.nxt:
                    wait(act, var_done, n + 2)
                    wait(act, r1_out, n + 1)
                    std(var_ps, std1, std1_out, 1.0)
                if st.nxt2:
                    m = n + 2
                    wait(act, xT_done, m + 1)
                    wait(act, z_done, m)
                    act.activation(xT[:, :], turn_ps[:, :], ACT.Copy).then_inc(xT_out, 1)
                if st.prep:
                    b = st.seq(2)
                    wait(act, pt_done, b + 1)
                    wait(act, p_done, b)
                    act.activation(PT_sb[:, :], prep_ps[:, 0:XW], ACT.Copy).then_inc(PT_out, 1)
                if st.nxt:
                    wait(act, st2_out, n + 2)
                    wait(act, r2_out, n + 1)
                    std(two(st2, 2), std2, std2_out, 1.0 / C)
                if st.prep:
                    b = st.seq(2)
                    wait(act, p_done, b + 1)
                    wait(act, z_done, b * 2)
                    act.activation(P_sb[:, 0:C + 1], prep_ps[:, 0:C + 1], ACT.Copy).then_inc(P_out, 1)
                if st.gram:
                    b = st.seq(3)
                    wait(act, gram_done, b + 1)
                    wait(act, ev_done, b)
                    wait(act, EV_out, b)
                    act.activation(G_sb[:, :], prep_ps[:, 0:XW], ACT.Copy).then_inc(G_out, 1)
                if st.nxt:
                    m = n + 1
                    wait(act, x1T_done, m + 1)
                    wait(act, up_done, m * FCH)
                    wait(act, x1lo_out, m)
                    act.activation(x1T_hi[:, :], turn_ps[:, :], ACT.Copy).then_inc(x1hi_out, 1)
                if st.prev:
                    wait(act, st4_out, n)
                    std(two(st4, 2), std4, std4_out, 1.0 / C)

            run_steps(act, body)

        @block.vector
        def _(dve):
            dve.wait_ge(consts, 1)
            dve.wait_ge(kv_turned, 1)
            dve.tensor_tensor(A_kv[:, 0:2, :], kv_ps[:, 0:2, :], rows(ident[:, :], 2), ALU.add)
            dve.tensor_tensor(A_kv[:, 2, :], kv_ps[:, 0, :], ident[:, :], ALU.add)
            dve.tensor_tensor(A_kv[:, 3:5, :], kv_ps[:, 2:4, :], rows(ident[:, :], 2), ALU.add).then_inc(A_ready, 1)
            dve.wait_ge(consts, 3)
            dve.tensor_tensor(center[:, :], center[:, :], ident[:, :], ALU.add)
            dve.wait_ge(bv_loaded, 16 * 3)
            dve.tensor_scalar(nbv_rows[:, :, :], bv_rows[:, 1:3, :], float(SEQ), None, ALU.mult).then_inc(nbv_ready, 1)

            def factors():
                dve.wait_ge(attn_rows, ATTN_ROWS)
                for i in range(4):
                    dve.tensor_scalar(gmask[:, i, :], head_mask[:, :], gcols[:, i:i + 1], 1.0 / (SEQ * SEQ), ALU.mult, ALU.mult)
                dve.wait_ge(qo_loaded, 16 * 2)
                dve.tensor_tensor(AqT[:, 0:C], w_raw[:, 5, :], ident[:, :], ALU.add).then_inc(masks_ready, 1)

            def u_row():
                dve.wait_ge(u_done, 1)
                dve.wait_ge(ln_loaded, 16 * 3)
                dve.tensor_tensor(u_rows[:, :], y_ps[:, 0:C], bo_rows[:, :], ALU.add).then_inc(u_ready, 1)

            def stats(t, st, done):
                for i in range(TILES // 2):
                    last = dve.bn_stats(st[:, i, :], pairs(t, i))
                last.then_inc(done, 1)

            def normalize(dst, src, st, rstd, done):
                for t in range(TILES):
                    last = dve.tensor_scalar(dst[:, t, :], src[:, t, :], st[:, t // 2, 3 * (t % 2) + 1:3 * (t % 2) + 2],
                                             rstd[:, t:t + 1], ALU.subtract, ALU.mult)
                last.then_inc(done, 1)

            def body(st):
                n, s = st.n, st.s
                if st.prep:
                    b = st.seq(2)
                    if st.c == -2:
                        dve.wait_ge(nbv_ready, 1)
                    wait(dve, ev_done, b + 1)
                    wait(dve, s_done, b)
                    wait(dve, M_out, b * 2)
                    dve.scalar_tensor_tensor(out=E_sb[:, :, :].rearrange("p j c -> p (j c)"),
                                             in0=bv_rows[:, 0:2, :].rearrange("p j c -> p (j c)"),
                                             scalar=G_sb[:, C:C + 1], in1=prep_ps[:, 0:256],
                                             op0=ALU.mult, op1=ALU.add)
                    dve.tensor_tensor(V_sb[:, :, :].rearrange("p j c -> p (j c)"), prep_ps[:, 256:512],
                                      nbv_rows[:, :, :].rearrange("p j c -> p (j c)"), ALU.add).then_inc(EV_out, 1)
                if st.prev:
                    wait(dve, down_done, n)
                    wait(dve, x1b2_out, n)
                    dve.tensor_tensor(y2[:, :, :], down_ps[:, :].rearrange("p (t c) -> p t c", c=C),
                                      x1b2[(s - 1) % 2][:, :, :], ALU.add).then_inc(y2_out, 1)
                    wait(dve, y2_out, n)
                    stats(y2, st3, st3_out)
                if st.prep:
                    b = st.seq(2)
                    if st.c == -2:
                        dve.wait_ge(bk_loaded, 16 * 2)
                    wait(dve, EV_out, b + 1)
                    wait(dve, s_done, b + 1)
                    for j in range(2):
                        last = dve.scalar_tensor_tensor(out=S_sb[:, j, :], in0=V_sb[:, 1 - j, :],
                                                        scalar=cols[:, j:j + 1],
                                                        in1=prep_ps[:, j * 128:(j + 1) * 128],
                                                        op0=ALU.mult, op1=ALU.add)
                    last.then_inc(S_out, 1)
                if st.c == -2:
                    factors()
                    u_row()
                if st.c == -1:
                    dve.wait_ge(ffn_rows, FFN_ROWS)
                    dve.tensor_copy(w1_hi[:, :], w1_sb[:, :]).then_inc(w1_split, 1)
                    dve.wait_ge(w1_split, 1)
                    dve.tensor_tensor(w1_lo[:, :], w1_sb[:, :], w1_hi[:, :].bitcast(f32), ALU.subtract).then_inc(w1_split, 1)
                if st.prev:
                    wait(dve, std3_out, n)
                    dve.reciprocal(rstd3[:, :], std3[:, :]).then_inc(r3_out, 1)
                    wait(dve, r3_out, n)
                    normalize(y2n, y2, st3, rstd3, y2n_out)
                if st.prev2:
                    wait(dve, std4_out, n - 1)
                    dve.reciprocal(rstd4[:, :], std4[:, :]).then_inc(r4_out, 1)
                    wait(dve, r4_out, n - 1)
                    wait(dve, res_free[s % 2], st.seq(-2) * 16 + 16)
                    normalize(res[s % 2], y3, st4, rstd4, res_out)
                if st.c == -2:
                    dve.wait_ge(masks_ready, 1)
                    prepare(dve, 1)
                if st.nxt:
                    m = n + 1
                    wait(dve, std1_out, m + 1)
                    dve.reciprocal(rstd1[:, :], std1[:, :]).then_inc(r1_out, 1)
                    wait(dve, r1_out, m + 1)
                    wait(dve, y_done, m + 1)
                    wait(dve, xu_out, m + 1)
                    for t in range(TILES):
                        last = dve.scalar_tensor_tensor(out=y1[:, t, :], in0=y_ps[:, t * C:(t + 1) * C],
                                                        scalar=rstd1[:, t:t + 1], in1=xu[(s + 1) % 2][:, t, :],
                                                        op0=ALU.mult, op1=ALU.add)
                    last.then_inc(y1_out, 1)
                    wait(dve, y1_out, m + 1)
                    stats(y1, st2, st2_out)
                if st.nxt:
                    m = n + 1
                    wait(dve, std2_out, m + 1)
                    dve.reciprocal(rstd2[:, :], std2[:, :]).then_inc(r2_out, 1)
                    wait(dve, r2_out, m + 1)
                    wait(dve, x1T_done, m)
                    wait(dve, x1beta_out, m)
                    normalize(x1, y1, st2, rstd2, x1_out)
                if st.c == GROUPS:
                    wait(dve, y2n_out, n)
                    dve.tensor_tensor(y2g[:, :, :], y2n[:, :, :], rows(gamma_rows[:, :]), ALU.mult).then_inc(y2g_out, 1)
                    wait(dve, y2g_out, n)
                    dve.tensor_tensor(y3[:, :, :], y2g[:, :, :], x1beta[(s - 1) % 2][:, :, :], ALU.add).then_inc(y3_out, 1)
                if st.prev:
                    wait(dve, y3_out, n)
                    stats(y3, st4, st4_out)
                if st.nxt:
                    m = n + 1
                    wait(dve, x1hi_out, m + 1)
                    wait(dve, up_done, m * FCH)
                    dve.tensor_tensor(x1T_lo[:, :], turn_ps[:, :], x1T_hi[:, :].bitcast(f32), ALU.subtract).then_inc(x1lo_out, 1)

            run_steps(dve, body)

        @block.tensor
        def _(pe):
            def mm(o, lhsT, rhs, start=True, stop=True, **kw):
                return pe.matmul(o, lhsT, rhs, start=start, stop=stop, **kw)

            def turn_kv():
                pe.wait_ge(consts, 1)
                pe.wait_ge(kv_loaded, 16 * 4)
                for i in range(4):
                    last = pe.transpose(kv_ps[:, i, :], w_raw[:, i, :], ident[:, :])
                last.then_inc(kv_turned, 1)

            def turn_o():
                pe.wait_ge(qo_loaded, 16 * 2)
                pe.transpose(down_ps[:, 0:128], w_raw[:, 4, :], ident[:, :]).then_inc(o_turned, 1)
                pe.wait_ge(lnb_ready, 1)
                pe.wait_ge(WoT_ready, 2)
                mm(y_ps[:, 0:C], lnb_wide[:, :], WoT[:, :]).then_inc(u_done, 1)

            def gram(b1_, m, slot):
                wait(pe, x_loaded[slot], m)
                wait(pe, P_out, b1_ - 1)
                for t in range(SEQ_TILES):
                    last = mm(prep_ps[:, 0:XW], X[slot][:, t, 0:C], X[slot][:, t, :],
                              start=(t == 0), stop=(t == SEQ_TILES - 1))
                last.then_inc(gram_done, 1)

            def up(n, k):
                if isinstance(n, int) and n == 0:
                    pe.wait_ge(w1_split, 2)
                wait(pe, x1hi_out, n + 1)
                if k >= 3:
                    wait(pe, relu_out, n * FCH + (k - 2))
                part = slice(k * 128, (k + 1) * 128)
                mm(up_ps[k % 3][:, :], w1_hi[:, part], x1T_hi[:, :], start=True, stop=False)
                mm(up_ps[k % 3][:, :], w1_lo[:, part], x1T_hi[:, :], start=False, stop=False)
                wait(pe, x1lo_out, n + 1)
                mm(up_ps[k % 3][:, :], w1_hi[:, part], x1T_lo[:, :], start=False, stop=True).then_inc(up_done, 1)

            def attention_matrix(b):
                wait(pe, M_out, (b + 1) * 2)
                mm(prep_ps[:, 0:XW], M_sb[:, :], AqT[:, :], start=True, stop=False)
                mm(prep_ps[:, C:C + 1], S12g[:, 1, :], ones[:, 0:1], start=False, stop=True).then_inc(pt_done, 1)

            def body(st):
                n, s = st.n, st.s
                if st.c == -2:
                    turn_kv()
                    pe.wait_ge(consts, 2)
                    gram(1, 16, 0)
                    pe.wait_ge(A_ready, 1)
                if st.prep:
                    b = st.seq(2)
                    wait(pe, G_out, b + 1)
                    mm(prep_ps[:, 0:256], G_sb[:, 0:C], A_kv[:, 0:2, :].rearrange("p j c -> p (j c)"))
                    mm(prep_ps[:, 256:512], G_sb[:, C:C + 1].to_broadcast([128, 128]),
                       A_kv[:, 1:3, :].rearrange("p j c -> p (j c)")).then_inc(ev_done, 1)
                if st.c == -2:
                    turn_o()
                if st.nxt:
                    m = n + 1
                    wait(pe, xT_out, m + 1)
                    wait(pe, P_out, st.seq(1) + 1)
                    wait(pe, std1_out, m)
                    mm(z_ps[:, :], P_sb[:, 0:C], xT[:, :]).then_inc(z_done, 1)
                if st.cur:
                    up(n, 0)
                    up(n, 1)
                if st.prep:
                    b = st.seq(2)
                    wait(pe, EV_out, b + 1)
                    for j in range(2):
                        last = mm(prep_ps[:, j * 128:(j + 1) * 128], A_kv[:, 3 + j, :], E_sb[:, j, :])
                    last.then_inc(s_done, 1)
                if st.cur:
                    up(n, 2)
                    up(n, 3)
                if st.nxt:
                    m = n + 1
                    wait(pe, z_out, m + 1)
                    wait(pe, sq_out, m + 1)
                    for t in range(TILES):
                        last = mm(z_ps[:, t:t + 1], zT_sq[:, t * TILE:(t + 1) * TILE], inv_c[:, :])
                    last.then_inc(var_done, 1)
                    wait(pe, y1_out, m)
                    for t in range(TILES):
                        last = mm(y_ps[:, t * C:(t + 1) * C], zT[:, t * TILE:(t + 1) * TILE], Wog[:, :])
                    last.then_inc(y_done, 1)
                if st.c == -2:
                    pe.wait_ge(masks_ready, 1)
                if st.c == -1:
                    pe.wait_ge(u_ready, 1)
                if st.nxt2:
                    m = n + 2
                    slot, g = st.slot(2), s % 2
                    wait(pe, x_loaded[slot], st.loads(2))
                    wait(pe, x1lo_out, n + 1)
                    for t in range(TILES):
                        last = pe.transpose(turn_ps[:, t * TILE:(t + 1) * TILE], X[slot][:, g * TILES + t, 0:C], ident[:, :])
                    last.then_inc(xT_done, 1)
                if st.cur:
                    wait(pe, relu_out, n * FCH + FCH)
                    wait(pe, y2_out, n)
                    for t in range(TILES):
                        if t == 2 and st.prep:
                            attention_matrix(st.seq(2))
                        for k in range(FCH):
                            last = mm(down_ps[:, t * C:(t + 1) * C], hT[:, k, t * TILE:(t + 1) * TILE], w2_sb[:, k, :],
                                      start=(k == 0), stop=(k == FCH - 1))
                    last.then_inc(down_done, 1)
                elif st.prep:
                    attention_matrix(st.seq(2))
                if st.prep:
                    b = st.seq(2)
                    wait(pe, PT_out, b + 1)
                    mm(prep_ps[:, 0:C], PT_sb[:, 0:C], center[:, :])
                    mm(prep_ps[:, C:C + 1], center[:, :], PT_sb[:, C:C + 1]).then_inc(p_done, 1)
                if st.gram:
                    gram(st.seq(3) + 1, st.loads(3), st.slot(3))
                if st.nxt:
                    m = n + 1
                    wait(pe, x1_out, m + 1)
                    wait(pe, xT_out, min(n + 3, GROUPS) if isinstance(n, int) else n + 3)
                    for t in range(TILES):
                        last = pe.transpose(turn_ps[:, t * TILE:(t + 1) * TILE], x1[:, t, :], ident[:, :])
                    last.then_inc(x1T_done, 1)

            run_steps(pe, body)


_ATTN = ['x', 'Wq', 'bq', 'Wk1', 'bk1', 'Wk2', 'bk2', 'Wv1', 'bv1', 'Wv2', 'bv2', 'g1', 'g2', 'g3', 'g4',
         'ln_g', 'ln_b', 'Wo', 'bo']
_FFN = ['w1', 'b1', 'w2', 'b2', 'gamma', 'beta']
_INS = ['L0_attn_' + n for n in _ATTN] + ['L0_ffn_' + n for n in _FFN]


def kernel(**inputs):
    import numpy as _np
    import concourse.bacc as _bacc
    from concourse import mybir as _mybir
    from concourse.bass_utils import run_bass_kernel_spmd as _run

    nc = _bacc.Bacc("TRN2", target_bir_lowering=False, num_devices=1)
    arrays, args = {}, []
    for name in _INS:
        a = _np.ascontiguousarray(inputs[name])
        arrays[f"in_{name}"] = a
        args.append(nc.dram_tensor(f"in_{name}", a.shape, _mybir.dt.from_np(a.dtype), kind="ExternalInput").ap())
    out = nc.dram_tensor("out_0", (BATCHES, SEQ, C), _mybir.dt.float32, kind="ExternalOutput").ap()
    build(nc, *args, out)
    r = _run(nc, [arrays], core_ids=[0])
    return r.results[0]["out_0"]
```

```python
from contextlib import ExitStack

import concourse.bass as bass
from concourse import mybir

BATCHES, SEQ, C, HEADS, FF = 8, 1024, 128, 16, 512
HEAD = C // HEADS
EPS = 1e-5
TILE = 128
SEQ_TILES = SEQ // TILE
TILES = 4
GROUP = TILES * TILE
SEQ_GROUPS = SEQ // GROUP
GROUPS = BATCHES * SEQ_GROUPS
FCH = FF // 128
XW = C + 2
PERIOD = 4


def build(nc, x, Wq, bq, Wk1, bk1, Wk2, bk2, Wv1, bv1, Wv2, bv2, g1, g2, g3, g4, ln_g, ln_b, Wo, bo,
          w1, b1, w2, b2, gamma, beta, out):
    f32 = mybir.dt.float32
    f32r = mybir.dt.float32r
    ALU = mybir.AluOpType
    ACT = mybir.ActivationFunctionType

    x_v = x.rearrange("b (p t) c -> b p t c", t=SEQ_TILES)
    out_v = out.rearrange("b (p t) c -> b p t c", t=SEQ_TILES)

    ctx = ExitStack()
    with ctx:
        def sb(name, shape, dt=f32):
            return ctx.enter_context(nc.sbuf_tensor(name, shape, dt))

        def bank(name):
            return ctx.enter_context(nc.psum_tensor(name, [128, 512], f32))

        def sem(name):
            return ctx.enter_context(nc.semaphore(name))

        ident = sb("ident", [128, 128])
        ones = sb("ones", [128, 128])
        center = sb("center", [128, 2, 128])
        spread64 = sb("spread64", [128, 128], f32r)
        head_mask = sb("head_mask", [128, 128])
        w_raw = sb("w_raw", [128, 6, 128])
        AqT = sb("AqT", [128, XW])
        A_kv = sb("A_kv", [128, 5, 128])
        WoT = sb("WoT", [128, 128])
        Wog = sb("Wog", [128, 128])
        bv_rows = sb("bv_rows", [128, 3, 128])
        nbv_rows = sb("nbv_rows", [128, 2, 128])
        cols = sb("cols", [128, 4])
        gcols = sb("gcols", [128, 4])
        gmask = sb("gmask", [128, 4, 128])
        lnb_wide = sb("lnb_wide", [128, 128])
        bo_rows = sb("bo_rows", [128, 128])
        u_rows = sb("u_rows", [128, 128])
        w1_sb = sb("w1_sb", [128, FF])
        w1_hi = sb("w1_hi", [128, FF], f32r)
        w1_lo = sb("w1_lo", [128, FF], f32r)
        b1_sb = sb("b1_sb", [128, FCH])
        w2_sb = sb("w2_sb", [128, FCH, C])
        b2_rows = sb("b2_rows", [128, C])
        gamma_rows = sb("gamma_rows", [128, C])
        beta_rows = sb("beta_rows", [128, C])
        eps_col = sb("eps_col", [128, 1])
        warm = sb("warm", [128, 1])

        X = [sb(f"X{i}", [128, SEQ_TILES, XW]) for i in range(2)]
        G_sb = sb("G_sb", [128, XW])
        E_sb = sb("E_sb", [128, 2, 128])
        V_sb = sb("V_sb", [128, 2, 128])
        S_sb = sb("S_sb", [128, 2, 128])
        gv = sb("gv", [128, 2, 128])
        T_sb = sb("T_sb", [128, 2, 128])
        S12 = sb("S12", [128, 128])
        S12g = sb("S12g", [128, 2, 128])
        M_half = sb("M_half", [128, 128])
        M_sb = sb("M_sb", [128, 128])
        PT_sb = sb("PT_sb", [128, XW])
        PQ_hi = sb("PQ_hi", [128, 512], f32r)
        PQ_lo = sb("PQ_lo", [128, 256], f32r)

        xT_hi = sb("xT_hi", [128, GROUP], f32r)
        xT_lo = sb("xT_lo", [128, GROUP], f32r)
        z_sq = sb("z_sq", [128, TILES, C])
        z_sum = sb("z_sum", [128, TILES])
        xu = [sb(f"xu{i}", [128, TILES, C]) for i in range(2)]
        std1 = sb("std1", [128, TILES])
        rstd1 = sb("rstd1", [128, TILES])
        y1 = sb("y1", [128, TILES, C])
        st2 = sb("st2", [128, TILES // 2, 6])
        std2 = sb("std2", [128, TILES])
        rstd2 = sb("rstd2", [128, TILES])
        x1 = sb("x1", [128, TILES, C])
        x1T_hi = sb("x1T_hi", [128, GROUP], f32r)
        x1T_lo = sb("x1T_lo", [128, GROUP], f32r)
        x1b2 = [sb(f"x1b2{i}", [128, TILES, C]) for i in range(2)]
        x1beta = [sb(f"x1beta{i}", [128, TILES, C]) for i in range(2)]
        hT = sb("hT", [128, FCH, GROUP])
        y2 = sb("y2", [128, TILES, C])
        st3 = sb("st3", [128, TILES // 2, 6])
        std3 = sb("std3", [128, TILES])
        rstd3 = sb("rstd3", [128, TILES])
        y2n = sb("y2n", [128, TILES, C])
        y2g = sb("y2g", [128, TILES, C])
        y3 = [sb(f"y3{i}", [128, TILES, C]) for i in range(2)]
        st4 = sb("st4", [128, TILES // 2, 6])
        std4 = sb("std4", [128, TILES])
        rstd4 = sb("rstd4", [128, TILES])
        nb4 = sb("nb4", [128, TILES])
        res = [sb(f"res{i}", [128, TILES, C]) for i in range(2)]

        turn_ps = bank("turn_ps")
        z_ps = [bank("z_ps0"), bank("z_ps1")]
        up_ps = [bank("up_ps0"), bank("up_ps1"), bank("up_ps2")]
        down_ps = bank("down_ps")
        prep_ps = bank("prep_ps")
        last_ps = [down_ps[:, 0:2 * C], prep_ps[:, 0:2 * C]]
        early_ps = up_ps[2]
        kv_ps = turn_ps[:, :].rearrange("p (j c) -> p j c", c=128)

        kv_loaded = sem("kv_loaded")
        bv_loaded = sem("bv_loaded")
        bk_loaded = sem("bk_loaded")
        ln_loaded = sem("ln_loaded")
        qo_loaded = sem("qo_loaded")
        attn_rows = sem("attn_rows")
        ffn_rows = sem("ffn_rows")
        x_loaded = [sem("x_loaded0"), sem("x_loaded1")]
        res_free = [sem("res_free0"), sem("res_free1")]
        const_set = sem("const_set")
        consts = sem("consts")
        kv_turned = sem("kv_turned")
        o_turned = sem("o_turned")
        lnb_ready = sem("lnb_ready")
        WoT_ready = sem("WoT_ready")
        A_ready = sem("A_ready")
        nbv_ready = sem("nbv_ready")
        u_done = sem("u_done")
        zw_done = sem("zw_done")
        zw_ready = sem("zw_ready")
        masks_ready = sem("masks_ready")
        u_ready = sem("u_ready")
        gram_done = sem("gram_done")
        ev_done = sem("ev_done")
        s_done = sem("s_done")
        pt_done = sem("pt_done")
        p_done = sem("p_done")
        xT_done = sem("xT_done")
        z_done = sem("z_done")
        x1T_done = sem("x1T_done")
        up_done = sem("up_done")
        down_done = sem("down_done")
        G_out = sem("G_out")
        PT_out = sem("PT_out")
        PQhi_out = sem("PQhi_out")
        xThi_out = sem("xThi_out")
        sq_out = sem("sq_out")
        std1_out = sem("std1_out")
        std2_out = sem("std2_out")
        std3_out = sem("std3_out")
        std4_out = sem("std4_out")
        x1hi_out = sem("x1hi_out")
        relu_out = sem("relu_out")
        EV_out = sem("EV_out")
        S_out = sem("S_out")
        w1_split = sem("w1_split")
        x1lo_out = sem("x1lo_out")
        xTlo_out = sem("xTlo_out")
        PQlo_out = sem("PQlo_out")
        r1_out = sem("r1_out")
        y1_out = sem("y1_out")
        st2_out = sem("st2_out")
        r2_out = sem("r2_out")
        x1_out = sem("x1_out")
        y2_out = sem("y2_out")
        st3_out = sem("st3_out")
        r3_out = sem("r3_out")
        y2n_out = sem("y2n_out")
        st4_out = sem("st4_out")
        r4_out = sem("r4_out")
        nb4_out = sem("nb4_out")
        res_out = sem("res_out")
        end_y2 = sem("end_y2")
        end_st3 = sem("end_st3")
        end_std3 = sem("end_std3")
        end_r3 = sem("end_r3")
        end_y2n = sem("end_y2n")
        end_y2g = [sem("end_y2g0"), sem("end_y2g1")]
        end_y3 = [sem("end_y30"), sem("end_y31")]
        end_st4 = sem("end_st4")
        end_std4 = sem("end_std4")
        end_r4 = sem("end_r4")
        end_res = sem("end_res")
        xu_out = sem("xu_out")
        m_step = sem("m_step")
        M_out = sem("M_out")
        x1b2_out = sem("x1b2_out")
        x1beta_out = sem("x1beta_out")
        y2g_out = sem("y2g_out")
        y3_out = sem("y3_out")

        def wait(eng, s, value):
            if isinstance(value, int) and value <= 0:
                return
            eng.wait_ge(s, value)

        def two(stats, k):
            return stats[:, :, k:6:3]

        def pairs(t, i):
            return t[:, 2 * i:2 * i + 2, :].rearrange("p t c -> p c t")

        def column(v):
            return v.rearrange("(p o) -> p o", o=1)

        def spread(v):
            return v.rearrange("(o c) -> o c", o=1).to_broadcast([128, C])

        def gram_bank(b):
            return early_ps if isinstance(b, int) and b == 1 else prep_ps

        def rows(t, n=TILES):
            return t.unsqueeze(1).to_broadcast([128, n, 128])

        def half_y3(eng, h):
            two_tiles, own = slice(2 * h, 2 * h + 2), (GROUPS - 1) % 2
            eng.wait_ge(end_y2n, h + 1)
            eng.tensor_tensor(y2g[:, two_tiles, :], y2n[:, two_tiles, :], rows(gamma_rows[:, :], 2), ALU.mult).then_inc(end_y2g[h], 1)
            eng.wait_ge(end_y2g[h], 1)
            eng.wait_ge(x1beta_out, GROUPS)
            eng.tensor_tensor(y3[own][:, two_tiles, :], y2g[:, two_tiles, :], x1beta[own][:, two_tiles, :], ALU.add).then_inc(end_y3[h], 1)

        def prepare(eng, b):
            wait(eng, EV_out, b + 1)
            wait(eng, pt_done, b)
            k = b * 4
            eng.tensor_tensor(gv[:, :, :], V_sb[:, :, :], gmask[:, 0:2, :], ALU.mult).then_inc(m_step, 1)
            wait(eng, S_out, b + 1)
            eng.tensor_tensor(S12[:, :], S_sb[:, 0, :], S_sb[:, 1, :], ALU.mult).then_inc(m_step, 1)
            wait(eng, m_step, k + 2)
            eng.tensor_tensor(T_sb[:, :, :], S_sb[:, :, :], gv[:, :, :], ALU.mult).then_inc(m_step, 1)
            eng.tensor_tensor(S12g[:, :, :], rows(S12[:, :], 2), gmask[:, 2:4, :], ALU.mult).then_inc(m_step, 1)
            wait(eng, m_step, k + 4)
            eng.tensor_tensor(M_half[:, :], T_sb[:, 0, :], T_sb[:, 1, :], ALU.add).then_inc(M_out, 1)
            wait(eng, M_out, b * 2 + 1)
            eng.tensor_tensor(M_sb[:, :], M_half[:, :], S12g[:, 0, :], ALU.add).then_inc(M_out, 1)

        class Step:
            def __init__(self, c, i=None):
                self.c, self.i = c, i
                self.s = c % PERIOD
                self.n = c if i is None else i * PERIOD + c

                def has(k):
                    return i is not None or 0 <= c + k < GROUPS

                self.cur, self.prev, self.prev2 = has(0), has(-1), has(-2)
                self.last = i is None and c == GROUPS - 1
                self.nxt, self.nxt2 = has(1), has(2)
                self.prep = c == -1 or (c != 0 and c % 2 == 0 and has(2))
                self.gram = c != -1 and c % 2 == 1 and has(3)

            def prepared(self):
                return 1 if self.c == -1 else self.seq(2)

            def seq(self, k):
                q = (self.c + k) // SEQ_GROUPS
                return q if self.i is None else self.i * (PERIOD // SEQ_GROUPS) + q

            def slot(self, k):
                return ((self.s + k) // SEQ_GROUPS) % 2

            def loads(self, k):
                q = (self.c + k) // PERIOD + 1
                return 16 * q if self.i is None else (self.i + q) * 16

        def run_steps(eng, body):
            first, loops = 2, (GROUPS - 5) // PERIOD
            for c in range(-2, first):
                body(Step(c))
            with eng.Fori(0, loops) as i:
                for c in range(first, first + PERIOD):
                    body(Step(c, i))
            for c in range(first + loops * PERIOD, GROUPS):
                body(Step(c))

        ATTN_ROWS = 16 * (4 + 1)
        FFN_ROWS = 16 * 6

        block = ctx.enter_context(nc.Block())

        @block.sync
        def _(sp):
            def load_x(b, slot):
                sp.dma_start(X[slot][:, :, 0:C], x_v[b, :, :, :]).then_inc(x_loaded[slot], 16)

            for g in range(SEQ_GROUPS):
                sp.sem_inc(res_free[g], 16)
            load_x(0, 0)
            for i, v in enumerate((bv1, bv2, bv1)):
                sp.dma_start(bv_rows[:, i, :], spread(v)).then_inc(bv_loaded, 16)
            for i, g in enumerate((g1, g3, g4, g2)):
                sp.dma_start(gcols[:, i:i + 1],
                             g.rearrange("(h o) -> h o", o=1).to_broadcast([HEADS, HEAD])).then_inc(attn_rows, 16)
            sp.dma_start(AqT[:, C:C + 1], column(bq)).then_inc(attn_rows, 16)
            load_x(1, 1)

            def store(b):
                for g in range(1 if isinstance(b, int) and b == BATCHES - 1 else SEQ_GROUPS):
                    wait(sp, res_out, b * SEQ_GROUPS + (g + 1))
                    o = (out_v[b, :, :, :] if isinstance(b, int) else
                         out_v[bass.ds(b, 1), :, :, :].rearrange("o p t c -> (o p) t c"))
                    sp.dma_start(o[:, g * TILES:(g + 1) * TILES, :], res[g][:, :, :]).then_inc(res_free[g], 16)

            def reload(b, slot):
                wait(sp, xu_out, b * SEQ_GROUPS + SEQ_GROUPS)
                wait(sp, xT_done, b * SEQ_GROUPS + SEQ_GROUPS)
                sp.dma_start(X[slot][:, :, 0:C],
                             x_v[b + 2, :, :, :] if isinstance(b, int) else
                             x_v[bass.ds(b + 2, 1), :, :, :].rearrange("o p t c -> (o p) t c")
                             ).then_inc(x_loaded[slot], 16)

            reload(0, 0)
            reload(1, 1)
            store(0)
            with sp.Fori(0, (BATCHES - 4) // 2) as i:
                for k in range(2):
                    reload(i * 2 + (k + 2), k)
                    store(i * 2 + (k + 1))
            for b in range(BATCHES - 3, BATCHES):
                store(b)
            for h in range(2):
                t = TILES + 2 * h
                sp.wait_ge(end_res, h + 1)
                sp.dma_start(out_v[BATCHES - 1, :, t:t + 2, :], res[1][:, 2 * h:2 * h + 2, :]).then_inc(res_free[1], 16)
            sp.wait_ge(res_free[0], 16 * (BATCHES + 1))
            sp.wait_ge(res_free[1], 16 * (BATCHES + 2))

        @block.gpsimd
        def _(pool):
            pool.memset(ident[:, :], 0.0).then_inc(const_set, 1)
            pool.memset(head_mask[:, :], 1.0).then_inc(const_set, 1)
            pool.wait_ge(const_set, 1)
            pool.affine_select(out=ident[:, :], in_=ident[:, :], compare_op=ALU.not_equal, fill=1.0, base=0,
                               pattern=[[-1, 128]], channel_multiplier=1).then_inc(consts, 1)
            for i in range(2):
                pool.memset(X[i][:, :, C:C + 1], 1.0)
                pool.memset(X[i][:, :, C + 1:XW], 0.0)
            pool.memset(ones[:, :], 1.0)
            pool.memset(center[:, 0, :], -1.0 / C)
            pool.memset(eps_col[:, :], EPS)
            pool.memset(AqT[:, C + 1:XW], 0.0).then_inc(consts, 1)
            pool.wait_ge(const_set, 2)
            blocks = head_mask[:, :].rearrange("p (h j) -> p h j", j=HEAD)
            pool.affine_select(out=blocks, in_=blocks, compare_op=ALU.is_ge, fill=0.0, base=0,
                               pattern=[[-HEAD, HEADS], [0, HEAD]], channel_multiplier=1).then_inc(const_set, 1)
            pool.wait_ge(const_set, 3)
            pool.affine_select(out=blocks, in_=blocks, compare_op=ALU.is_ge, fill=0.0, base=HEAD - 1,
                               pattern=[[HEAD, HEADS], [0, HEAD]], channel_multiplier=-1).then_inc(consts, 1)
            for i, w in enumerate((Wo, Wq)):
                pool.dma_start(w_raw[:, 4 + i, :], w[:, :]).then_inc(qo_loaded, 16)
            for dst, v in ((cols[:, 0:1], bk1), (cols[:, 1:2], bk2)):
                pool.dma_start(dst, column(v)).then_inc(bk_loaded, 16)
            for dst, v in ((b2_rows, b2[0, :]), (beta_rows, beta), (gamma_rows, gamma)):
                pool.dma_start(dst[:, :], spread(v)).then_inc(ffn_rows, 16)
            pool.dma_start(w1_sb[:, :], w1[0, :, :]).then_inc(ffn_rows, 16)
            with nc.allow_non_contiguous_dma(reason="b1 by columns, once"):
                pool.dma_start(b1_sb[:, :], b1[0, :].rearrange("(k p) -> p k", p=128)).then_inc(ffn_rows, 16)
            pool.dma_start(w2_sb[:, :, :], w2[0, :, :].rearrange("(k p) c -> p k c", p=128)).then_inc(ffn_rows, 16)
            pool.wait_ge(masks_ready, 1)

            def body(st):
                n, s = st.n, st.s
                if st.prep and st.c >= 0:
                    prepare(pool, st.prepared())
                if st.prev and not st.last:
                    wait(pool, y2n_out, n)
                    pool.tensor_tensor(y2g[:, :, :], y2n[:, :, :], rows(gamma_rows[:, :]), ALU.mult).then_inc(y2g_out, 1)
                    wait(pool, y2g_out, n)
                    wait(pool, x1beta_out, n)
                    wait(pool, res_out, n - 2)
                    pool.tensor_tensor(y3[(s - 1) % 2][:, :, :], y2g[:, :, :], x1beta[(s - 1) % 2][:, :, :], ALU.add).then_inc(y3_out, 1)
                if st.nxt2:
                    m = n + 2
                    slot, g = st.slot(2), s % 2
                    wait(pool, x_loaded[slot], st.loads(2))
                    if st.c == -2:
                        pool.wait_ge(u_ready, 1)
                    wait(pool, y1_out, m - 1)
                    pool.tensor_tensor(xu[s % 2][:, :, :], X[slot][:, g * TILES:(g + 1) * TILES, 0:C],
                                       rows(u_rows[:, :]), ALU.add).then_inc(xu_out, 1)
                if st.c == -1:
                    prepare(pool, 1)
                if st.nxt:
                    m = n + 1
                    wait(pool, x1_out, m + 1)
                    if st.c == -1:
                        pool.wait_ge(ffn_rows, FFN_ROWS)
                    wait(pool, y2_out, m - 1)
                    pool.tensor_tensor(x1b2[(s + 1) % 2][:, :, :], x1[:, :, :], rows(b2_rows[:, :]), ALU.add).then_inc(x1b2_out, 1)
                    wait(pool, y3_out, m - 1)
                    pool.tensor_tensor(x1beta[(s + 1) % 2][:, :, :], x1[:, :, :], rows(beta_rows[:, :]), ALU.add).then_inc(x1beta_out, 1)

            run_steps(pool, body)
            half_y3(pool, 0)

        @block.scalar
        def _(act):
            for i, w in enumerate((Wv1, Wv2, Wk1, Wk2)):
                act.dma_start(w_raw[:, i, :], w[:, :]).then_inc(kv_loaded, 16)
            act.wait_ge(consts, 2)
            act.activation(warm[:, :], eps_col[:, :], ACT.Sqrt)
            for dst, v in ((cols[:, 2:3], column(ln_g)), (cols[:, 3:4], column(ln_b)), (bo_rows[:, :], spread(bo))):
                act.dma_start(dst, v).then_inc(ln_loaded, 16)
            act.activation(spread64[:, :], ones[:, :], ACT.Copy, scale=1.0 / 64)

            def output_weights():
                act.wait_ge(consts, 2)
                act.wait_ge(ln_loaded, 16 * 3)
                act.activation(lnb_wide[:, :], ones[:, :], ACT.Copy, scale=cols[:, 3:4]).then_inc(lnb_ready, 1)
                act.wait_ge(o_turned, 1)
                act.activation(WoT[:, :], down_ps[:, 0:128], ACT.Copy).then_inc(WoT_ready, 1)
                act.activation(Wog[:, :], down_ps[:, 0:128], ACT.Copy, scale=cols[:, 2:3]).then_inc(WoT_ready, 1)
                act.wait_ge(zw_done, 1)
                act.activation(center[:, 1, :], up_ps[1][:, 0:C], ACT.Copy).then_inc(zw_ready, 1)

            def std(src, dst, done, scale):
                act.activation(dst[:, :], src, ACT.Sqrt, bias=eps_col[:, :], scale=scale).then_inc(done, 1)

            def squares(m):
                wait(act, r1_out, m)
                for t in range(TILES):
                    if t % 2 == 0:
                        wait(act, z_done, m * 2 + (t // 2 + 1))
                    act.activation(z_sq[:, t, :], z_ps[t // 2][:, t % 2 * 256:t % 2 * 256 + C], ACT.Square,
                                   accum_out=z_sum[:, t:t + 1]).then_inc(sq_out, 1)
                wait(act, sq_out, m * TILES + TILES)
                std(z_sum[:, :], std1, std1_out, 1.0 / C)

            def PT_copy(b):
                wait(act, pt_done, b + 1)
                wait(act, p_done, b)
                act.activation(PT_sb[:, :], prep_ps[:, 0:XW], ACT.Copy).then_inc(PT_out, 1)

            def PQ_upper(b):
                wait(act, p_done, b + 1)
                wait(act, z_done, b * (SEQ_GROUPS * 2))
                act.activation(PQ_hi[:, :], prep_ps[:, :], ACT.Copy).then_inc(PQhi_out, 1)

            def result(m, buf, q):
                wait(act, nb4_out, m + 1)
                wait(act, res_free[buf], 16 * (q + 1))
                for t in range(TILES):
                    last = act.activation(res[buf][:, t, :], y3[buf][:, t, :], ACT.Identity,
                                          scale=rstd4[:, t:t + 1], bias=nb4[:, t:t + 1])
                last.then_inc(res_out, 1)

            def xT_upper(m):
                wait(act, xT_done, m + 1)
                wait(act, z_done, m * 2)
                wait(act, xTlo_out, m)
                act.activation(xT_hi[:, :], turn_ps[:, :], ACT.Copy).then_inc(xThi_out, 1)

            def gram_out(b):
                wait(act, gram_done, b + 1)
                wait(act, ev_done, b)
                wait(act, EV_out, b)
                act.activation(G_sb[:, :], gram_bank(b)[:, 0:XW], ACT.Copy).then_inc(G_out, 1)

            def relu(st, k):
                n = st.n
                wait(act, up_done, n * FCH + (k + 1))
                act.activation(hT[:, k, :], up_ps[k % len(up_ps)][:, :], ACT.Relu, bias=b1_sb[:, k:k + 1]).then_inc(relu_out, 1)

            def body(st):
                n, s = st.n, st.s
                if st.c == -2:
                    gram_out(0)
                    xT_upper(0)
                    output_weights()
                    gram_out(1)
                if st.nxt and st.c != 0:
                    squares(n + 1)
                if st.cur:
                    if st.c == 0:
                        act.wait_ge(ffn_rows, FFN_ROWS)
                    relu(st, 0)
                if st.prev:
                    wait(act, st3_out, n)
                    std(two(st3, 2), std3, std3_out, 1.0 / C)
                if st.cur:
                    relu(st, 1)
                    relu(st, 2)
                    relu(st, 3)
                if st.prev2:
                    wait(act, st4_out, n - 1)
                    std(two(st4, 2), std4, std4_out, 1.0 / C)
                if st.c == -1:
                    xT_upper(1)
                if st.nxt:
                    wait(act, st2_out, n + 2)
                    wait(act, r2_out, n + 1)
                    std(two(st2, 2), std2, std2_out, 1.0 / C)
                if st.nxt2 and st.c >= 0:
                    xT_upper(n + 2)
                if st.prep:
                    PT_copy(st.prepared())
                if st.c == -1:
                    squares(1)
                elif st.prep:
                    PQ_upper(st.prepared())
                if st.prev2:
                    result(n - 2, s % 2, st.seq(-2))
                if st.nxt:
                    m = n + 1
                    wait(act, x1T_done, m + 1)
                    wait(act, up_done, m * FCH)
                    wait(act, x1lo_out, m)
                    act.activation(x1T_hi[:, :], turn_ps[:, :], ACT.Copy).then_inc(x1hi_out, 1)
                if st.c == -1:
                    PQ_upper(1)
                if st.gram:
                    gram_out(st.seq(3))

            run_steps(act, body)

            def half_std(stats, dst, h, ready, done):
                act.wait_ge(ready, h + 1)
                act.activation(dst[:, 2 * h:2 * h + 2], stats[:, h, 2:6:3], ACT.Sqrt,
                               bias=eps_col[:, :], scale=1.0 / C).then_inc(done, 1)

            half_std(st3, std3, 0, end_st3, end_std3)
            act.wait_ge(st4_out, GROUPS - 1)
            std(two(st4, 2), std4, std4_out, 1.0 / C)
            half_std(st3, std3, 1, end_st3, end_std3)
            result(GROUPS - 2, GROUPS % 2, BATCHES - 1)
            half_std(st4, std4, 0, end_st4, end_std4)
            half_std(st4, std4, 1, end_st4, end_std4)

        @block.vector
        def _(dve):
            dve.wait_ge(consts, 1)
            dve.wait_ge(kv_turned, 1)
            dve.tensor_tensor(A_kv[:, 0:2, :], kv_ps[:, 0:2, :], rows(ident[:, :], 2), ALU.add)
            dve.tensor_tensor(A_kv[:, 2, :], kv_ps[:, 0, :], ident[:, :], ALU.add)
            dve.tensor_tensor(A_kv[:, 3:5, :], kv_ps[:, 2:4, :], rows(ident[:, :], 2), ALU.add).then_inc(A_ready, 1)
            dve.wait_ge(consts, 3)
            dve.tensor_tensor(center[:, 0, :], center[:, 0, :], ident[:, :], ALU.add)
            dve.wait_ge(bv_loaded, 16 * 3)
            dve.tensor_scalar(nbv_rows[:, :, :], bv_rows[:, 1:3, :], float(SEQ), None, ALU.mult).then_inc(nbv_ready, 1)

            def factors():
                dve.wait_ge(attn_rows, ATTN_ROWS)
                for i in range(4):
                    dve.tensor_scalar(gmask[:, i, :], head_mask[:, :], gcols[:, i:i + 1], 1.0 / (SEQ * SEQ), ALU.mult, ALU.mult)
                dve.wait_ge(qo_loaded, 16 * 2)
                dve.tensor_tensor(AqT[:, 0:C], w_raw[:, 5, :], ident[:, :], ALU.add).then_inc(masks_ready, 1)

            def u_row():
                dve.wait_ge(u_done, 1)
                dve.wait_ge(ln_loaded, 16 * 3)
                dve.tensor_tensor(u_rows[:, :], up_ps[0][:, 0:C], bo_rows[:, :], ALU.add).then_inc(u_ready, 1)

            def stats(t, st, done):
                for i in range(TILES // 2):
                    last = dve.bn_stats(st[:, i, :], pairs(t, i))
                last.then_inc(done, 1)

            def normalize(dst, src, st, rstd, done):
                for t in range(TILES):
                    last = dve.tensor_scalar(dst[:, t, :], src[:, t, :], st[:, t // 2, 3 * (t % 2) + 1:3 * (t % 2) + 2],
                                             rstd[:, t:t + 1], ALU.subtract, ALU.mult)
                last.then_inc(done, 1)

            def split_w1():
                dve.wait_ge(ffn_rows, FFN_ROWS)
                dve.tensor_copy(w1_hi[:, :], w1_sb[:, :]).then_inc(w1_split, 1)
                dve.wait_ge(w1_split, 1)
                dve.tensor_tensor(w1_lo[:, :], w1_sb[:, :], w1_hi[:, :].bitcast(f32), ALU.subtract).then_inc(w1_split, 1)

            def xT_rest(m):
                wait(dve, xThi_out, m + 1)
                dve.tensor_tensor(xT_lo[:, :], turn_ps[:, :], xT_hi[:, :].bitcast(f32), ALU.subtract).then_inc(xTlo_out, 1)

            def PQ_rest(b):
                wait(dve, PQhi_out, b + 1)
                dve.tensor_tensor(PQ_lo[:, :], prep_ps[:, 0:256], PQ_hi[:, 0:256].bitcast(f32), ALU.subtract)
                dve.tensor_tensor(PQ_hi[64:128, 256:512], prep_ps[64:128, 256:512],
                                  PQ_hi[64:128, 256:512].bitcast(f32), ALU.subtract).then_inc(PQlo_out, 1)

            def y3_stats(m, buf):
                wait(dve, y3_out, m + 1)
                stats(y3[buf], st4, st4_out)

            def result_factors(m):
                wait(dve, std4_out, m + 1)
                wait(dve, res_out, m)
                dve.reciprocal(rstd4[:, :], std4[:, :]).then_inc(r4_out, 1)
                wait(dve, r4_out, m + 1)
                dve.scalar_tensor_tensor(out=nb4[:, :].rearrange("p (i t) -> p i t", t=2), in0=two(st4, 1), scalar=-1.0,
                                         in1=rstd4[:, :].rearrange("p (i t) -> p i t", t=2),
                                         op0=ALU.mult, op1=ALU.mult).then_inc(nb4_out, 1)

            def add_y2(n, s):
                wait(dve, down_done, n + 1)
                wait(dve, x1b2_out, n + 1)
                dve.tensor_tensor(y2[:, :, :], down_ps[:, :].rearrange("p (t c) -> p t c", c=C),
                                  x1b2[s % 2][:, :, :], ALU.add).then_inc(y2_out, 1)

            def s_out(b):
                if isinstance(b, int) and b == 0:
                    dve.wait_ge(bk_loaded, 16 * 2)
                wait(dve, EV_out, b + 1)
                wait(dve, s_done, b + 1)
                for j in range(2):
                    last = dve.scalar_tensor_tensor(out=S_sb[:, j, :], in0=V_sb[:, 1 - j, :],
                                                    scalar=cols[:, j:j + 1],
                                                    in1=prep_ps[:, j * 128:(j + 1) * 128],
                                                    op0=ALU.mult, op1=ALU.add)
                last.then_inc(S_out, 1)

            def body(st):
                n, s = st.n, st.s
                if st.prep:
                    b = st.prepared()
                    if st.c == -2:
                        dve.wait_ge(nbv_ready, 1)
                    wait(dve, ev_done, b + 1)
                    wait(dve, s_done, b)
                    wait(dve, M_out, b * 2)
                    dve.scalar_tensor_tensor(out=E_sb[:, :, :].rearrange("p j c -> p (j c)"),
                                             in0=bv_rows[:, 0:2, :].rearrange("p j c -> p (j c)"),
                                             scalar=G_sb[:, C:C + 1], in1=gram_bank(b)[:, 0:256],
                                             op0=ALU.mult, op1=ALU.add)
                    dve.tensor_tensor(V_sb[:, :, :].rearrange("p j c -> p (j c)"), gram_bank(b)[:, 256:512],
                                      nbv_rows[:, :, :].rearrange("p j c -> p (j c)"), ALU.add).then_inc(EV_out, 1)
                if st.c == -2:
                    factors()
                if st.prev2:
                    y3_stats(n - 2, s % 2)
                if st.prep:
                    s_out(st.prepared())
                if st.c == -2:
                    dve.wait_ge(masks_ready, 1)
                    prepare(dve, 0)
                    xT_rest(0)
                    u_row()
                    split_w1()
                if st.nxt:
                    m = n + 1
                    wait(dve, std1_out, m + 1)
                    dve.reciprocal(rstd1[:, :], std1[:, :]).then_inc(r1_out, 1)
                    wait(dve, r1_out, m + 1)
                    wait(dve, xu_out, m + 1)
                    for t in range(TILES):
                        last = dve.scalar_tensor_tensor(out=y1[:, t, :], in0=z_ps[t // 2][:, t % 2 * 256 + C:t % 2 * 256 + 256],
                                                        scalar=rstd1[:, t:t + 1], in1=xu[(s + 1) % 2][:, t, :],
                                                        op0=ALU.mult, op1=ALU.add)
                    last.then_inc(y1_out, 1)
                    if st.c == -1:
                        xT_rest(1)
                    wait(dve, y1_out, m + 1)
                    stats(y1, st2, st2_out)
                if st.prev:
                    wait(dve, std3_out, n)
                    dve.reciprocal(rstd3[:, :], std3[:, :]).then_inc(r3_out, 1)
                    wait(dve, r3_out, n)
                    normalize(y2n, y2, st3, rstd3, y2n_out)
                if st.prev2:
                    result_factors(n - 2)
                if st.nxt2 and st.c >= 0:
                    xT_rest(n + 2)
                if st.nxt:
                    m = n + 1
                    wait(dve, std2_out, m + 1)
                    dve.reciprocal(rstd2[:, :], std2[:, :]).then_inc(r2_out, 1)
                    wait(dve, r2_out, m + 1)
                    wait(dve, x1T_done, m)
                    wait(dve, x1beta_out, m)
                    normalize(x1, y1, st2, rstd2, x1_out)
                if st.last:
                    wait(dve, y2n_out, n)
                    dve.tensor_tensor(y2g[:, :, :], y2n[:, :, :], rows(gamma_rows[:, :]), ALU.mult).then_inc(y2g_out, 1)
                    wait(dve, y2g_out, n)
                    wait(dve, res_out, n - 2)
                    dve.tensor_tensor(y3[(s - 1) % 2][:, :, :], y2g[:, :, :], x1beta[(s - 1) % 2][:, :, :], ALU.add).then_inc(y3_out, 1)
                if st.prep and st.c != -1:
                    PQ_rest(st.prepared())
                if st.cur and st.nxt2:
                    add_y2(n, s)
                if st.cur and not st.prep and st.nxt2:
                    wait(dve, y2_out, n + 1)
                    stats(y2, st3, st3_out)
                if st.nxt:
                    m = n + 1
                    wait(dve, x1hi_out, m + 1)
                    wait(dve, up_done, m * FCH)
                    dve.tensor_tensor(x1T_lo[:, :], turn_ps[:, :], x1T_hi[:, :].bitcast(f32), ALU.subtract).then_inc(x1lo_out, 1)
                if st.c == -1:
                    PQ_rest(1)
                if st.cur and not st.nxt2 and not st.last:
                    add_y2(n, s)
                if st.cur and (st.prep or not st.nxt2) and not st.last:
                    wait(dve, y2_out, n + 1)
                    stats(y2, st3, st3_out)

            run_steps(dve, body)

            half = [slice(0, 2), slice(2, 4)]
            own = (GROUPS - 1) % 2

            def half_y2(h):
                dve.wait_ge(down_done, GROUPS + h)
                dve.wait_ge(x1b2_out, GROUPS)
                dve.tensor_tensor(y2[:, half[h], :], last_ps[h].rearrange("p (t c) -> p t c", c=C),
                                  x1b2[own][:, half[h], :], ALU.add).then_inc(end_y2, 1)
                dve.wait_ge(end_y2, h + 1)
                dve.bn_stats(st3[:, h, :], pairs(y2, h)).then_inc(end_st3, 1)

            def half_y2n(h):
                dve.wait_ge(end_std3, h + 1)
                dve.reciprocal(rstd3[:, half[h]], std3[:, half[h]]).then_inc(end_r3, 1)
                dve.wait_ge(end_r3, h + 1)
                half_normalize(y2n, y2, st3, rstd3, h, end_y2n)

            def half_normalize(dst, src, st, rstd, h, done):
                for t in range(2 * h, 2 * h + 2):
                    last = dve.tensor_scalar(dst[:, t, :], src[:, t, :], st[:, h, 3 * (t % 2) + 1:3 * (t % 2) + 2],
                                             rstd[:, t:t + 1], ALU.subtract, ALU.mult)
                last.then_inc(done, 1)

            def half_st4(h):
                dve.wait_ge(end_y3[h], 1)
                dve.bn_stats(st4[:, h, :], pairs(y3[own], h)).then_inc(end_st4, 1)

            def half_res(h):
                dve.wait_ge(end_std4, h + 1)
                dve.wait_ge(res_out, GROUPS - 1)
                dve.reciprocal(rstd4[:, half[h]], std4[:, half[h]]).then_inc(end_r4, 1)
                dve.wait_ge(end_r4, h + 1)
                dve.wait_ge(res_free[own], 16 * BATCHES)
                half_normalize(res[own], y3[own], st4, rstd4, h, end_res)

            half_y2(0)
            y3_stats(GROUPS - 2, 1 - own)
            half_y2(1)
            result_factors(GROUPS - 2)
            half_y2n(0)
            half_y2n(1)
            half_y3(dve, 1)
            half_st4(0)
            half_st4(1)
            half_res(0)
            half_res(1)

        @block.tensor
        def _(pe):
            def mm(o, lhsT, rhs, start=True, stop=True):
                return pe.matmul(o, lhsT, rhs, start=start, stop=stop)

            def keep_warm(times):
                for _ in range(times):
                    mm(down_ps[:, 0:128], ident[:, :], ident[:, :])

            def turn_kv():
                pe.wait_ge(kv_loaded, 16 * 4)
                for i in range(4):
                    last = pe.transpose(kv_ps[:, i, :], w_raw[:, i, :], ident[:, :])
                last.then_inc(kv_turned, 1)

            def turn_o():
                pe.wait_ge(qo_loaded, 16 * 2)
                pe.transpose(down_ps[:, 0:128], w_raw[:, 4, :], ident[:, :]).then_inc(o_turned, 1)

            def output_rows():
                pe.wait_ge(lnb_ready, 1)
                pe.wait_ge(WoT_ready, 2)
                mm(up_ps[0][:, 0:C], lnb_wide[:, :], WoT[:, :]).then_inc(u_done, 1)
                pe.wait_ge(nbv_ready, 1)
                mm(up_ps[1][:, 0:C], center[:, 0, :], Wog[:, :]).then_inc(zw_done, 1)

            def gram(b, loads, slot, middle):
                wait(pe, x_loaded[slot], loads)
                bank = gram_bank(b)
                if bank is prep_ps:
                    wait(pe, PQlo_out, b)
                for t in range(SEQ_TILES):
                    if t == SEQ_TILES // 2:
                        middle()
                    last = mm(bank[:, 0:XW], X[slot][:, t, 0:C], X[slot][:, t, :],
                              start=(t == 0), stop=(t == SEQ_TILES - 1))
                last.then_inc(gram_done, 1)

            def up(n, k):
                if isinstance(n, int) and n == 0:
                    pe.wait_ge(w1_split, 2)
                wait(pe, x1hi_out, n + 1)
                if k >= len(up_ps):
                    wait(pe, relu_out, n * FCH + (k - len(up_ps) + 1))
                part = slice(k * 128, (k + 1) * 128)
                mm(up_ps[k % len(up_ps)][:, :], w1_hi[:, part], x1T_hi[:, :], start=True, stop=False)
                mm(up_ps[k % len(up_ps)][:, :], w1_lo[:, part], x1T_hi[:, :], start=False, stop=False)
                wait(pe, x1lo_out, n + 1)
                mm(up_ps[k % len(up_ps)][:, :], w1_hi[:, part], x1T_lo[:, :], start=False, stop=True).then_inc(up_done, 1)

            def gram_av(b):
                wait(pe, G_out, b + 1)
                mm(gram_bank(b)[:, 0:256], G_sb[:, 0:C], A_kv[:, 0:2, :].rearrange("p j c -> p (j c)"))
                mm(gram_bank(b)[:, 256:512], G_sb[:, C:C + 1].to_broadcast([128, 128]),
                   A_kv[:, 1:3, :].rearrange("p j c -> p (j c)")).then_inc(ev_done, 1)

            def attention_matrix(b):
                wait(pe, M_out, (b + 1) * 2)
                mm(prep_ps[:, 0:XW], M_sb[:, :], AqT[:, :], start=True, stop=False)
                mm(prep_ps[:, C:C + 1], S12g[:, 1, :], ones[:, 0:1], start=False, stop=True).then_inc(pt_done, 1)

            def centered(b):
                if isinstance(b, int) and b == 0:
                    pe.wait_ge(zw_ready, 1)
                wait(pe, PT_out, b + 1)
                both = center[:, :, :].rearrange("p j c -> p (j c)")
                mm(prep_ps[:, 0:256], PT_sb[:, 0:C], both)
                mm(prep_ps[:, 256:512], PT_sb[:, C:C + 1].to_broadcast([128, 128]), both).then_inc(p_done, 1)

            def ak_e(b):
                wait(pe, EV_out, b + 1)
                for j in range(2):
                    last = mm(prep_ps[:, j * 128:(j + 1) * 128], A_kv[:, 3 + j, :], E_sb[:, j, :])
                last.then_inc(s_done, 1)

            def turn_x1(m, more):
                wait(pe, x1_out, m + 1)
                wait(pe, xTlo_out, m + 2 if more else m + 1)
                for t in range(TILES):
                    last = pe.transpose(turn_ps[:, t * TILE:(t + 1) * TILE], x1[:, t, :], ident[:, :])
                last.then_inc(x1T_done, 1)

            def product(m, b, middle=None):
                wait(pe, PQlo_out, b + 1)
                wait(pe, y1_out, m)
                wait(pe, xTlo_out, m + 1)
                for t in range(TILES):
                    o = z_ps[t // 2][:, t % 2 * 256:t % 2 * 256 + 256]
                    part = slice(t * TILE, (t + 1) * TILE)
                    mm(o, spread64[:, :], PQ_hi[:, 256:512], start=True, stop=False)
                    mm(o, xT_hi[:, part], PQ_hi[:, 0:256], start=False, stop=False)
                    mm(o, xT_hi[:, part], PQ_lo[:, :], start=False, stop=False)
                    last = mm(o, xT_lo[:, part], PQ_hi[:, 0:256], start=False, stop=True)
                    if t % 2 == 1:
                        last.then_inc(z_done, 1)
                    if t == 1 and middle is not None:
                        middle()

            def turn_x(m, loads, slot, g):
                wait(pe, x_loaded[slot], loads)
                wait(pe, x1lo_out, m - 1)
                for t in range(TILES):
                    last = pe.transpose(turn_ps[:, t * TILE:(t + 1) * TILE], X[slot][:, g * TILES + t, 0:C], ident[:, :])
                last.then_inc(xT_done, 1)

            def body(st):
                n, s = st.n, st.s
                if st.c == -2:
                    pe.wait_ge(consts, 1)
                    keep_warm(8)
                    pe.wait_ge(consts, 2)
                    gram(0, 16, 0, turn_kv)
                    pe.wait_ge(A_ready, 1)
                    gram_av(0)
                    turn_x(0, 16, 0, 0)
                    turn_o()
                if st.c == -1:
                    gram_av(1)
                    product(0, 0, lambda: ak_e(1))
                elif st.nxt and st.c != 0:
                    product(n + 1, st.seq(1), (lambda: gram_av(st.prepared())) if st.prep else None)
                if st.cur:
                    up(n, 0)
                if st.prep and st.c != -1:
                    ak_e(st.prepared())
                if st.cur:
                    up(n, 1)
                    up(n, 2)
                    up(n, 3)
                if st.c == -2:
                    output_rows()
                    gram(1, 16, 1, lambda: None)
                elif st.nxt2:
                    turn_x(n + 2, st.loads(2), st.slot(2), s % 2)
                if st.c == -1:
                    keep_warm(9)
                    product(1, 0, lambda: attention_matrix(1))
                if st.cur:
                    wait(pe, y2_out, n)
                    for t in range(TILES):
                        to = last_ps[t // 2][:, t % 2 * C:(t % 2 + 1) * C] if st.last else down_ps[:, t * C:(t + 1) * C]
                        if t == 3 and st.nxt and not st.nxt2:
                            turn_x1(n + 1, False)
                        if t == 2 and st.prep:
                            attention_matrix(st.prepared())
                        for k in range(FCH):
                            if t == 2 and k == 2 and st.prep:
                                centered(st.prepared())
                            if t == 0:
                                wait(pe, relu_out, n * FCH + (k + 1))
                            last = mm(to, hT[:, k, t * TILE:(t + 1) * TILE], w2_sb[:, k, :],
                                      start=(k == 0), stop=(k == FCH - 1))
                        if t == 1 and st.last:
                            last.then_inc(down_done, 1)
                    last.then_inc(down_done, 1)
                if st.c == -2:
                    attention_matrix(0)
                    centered(0)
                if st.gram:
                    gram(st.seq(3), st.loads(3), st.slot(3), lambda: turn_x1(n + 1, True))
                elif st.nxt and st.nxt2:
                    turn_x1(n + 1, True)
                if st.c == -1:
                    centered(1)

            run_steps(pe, body)


_ATTN = ['x', 'Wq', 'bq', 'Wk1', 'bk1', 'Wk2', 'bk2', 'Wv1', 'bv1', 'Wv2', 'bv2', 'g1', 'g2', 'g3', 'g4',
         'ln_g', 'ln_b', 'Wo', 'bo']
_FFN = ['w1', 'b1', 'w2', 'b2', 'gamma', 'beta']
_INS = ['L0_attn_' + n for n in _ATTN] + ['L0_ffn_' + n for n in _FFN]


def kernel(**inputs):
    import numpy as _np
    import concourse.bacc as _bacc
    from concourse import mybir as _mybir
    from concourse.bass_utils import run_bass_kernel_spmd as _run

    nc = _bacc.Bacc("TRN2", target_bir_lowering=False, num_devices=1)
    arrays, args = {}, []
    for name in _INS:
        a = _np.ascontiguousarray(inputs[name])
        arrays[f"in_{name}"] = a
        args.append(nc.dram_tensor(f"in_{name}", a.shape, _mybir.dt.from_np(a.dtype), kind="ExternalInput").ap())
    out = nc.dram_tensor("out_0", (BATCHES, SEQ, C), _mybir.dt.float32, kind="ExternalOutput").ap()
    build(nc, *args, out)
    r = _run(nc, [arrays], core_ids=[0])
    return r.results[0]["out_0"]
```
